# Optimizing a Trainium2 kernel written in Bass

```python
import numpy as np
import jax
import jax.numpy as jnp

def _softmax(x, axis=-1):
    return jax.nn.softmax(x, axis=axis)

def _gelu(x):
    return jax.nn.gelu(x, approximate=True)

def _silu(x):
    return jax.nn.silu(x)

def _sigmoid(x):
    return jax.nn.sigmoid(x)

def _layernorm(x, axis=-1, eps=1e-05):
    m = jnp.mean(x, axis=axis, keepdims=True)
    v = jnp.var(x, axis=axis, keepdims=True)
    return (x - m) / jnp.sqrt(v + eps)

def _scatter_add(tgt, idx, src, axis=0):
    return tgt.at[idx].add(src)

def _segment_sum(src, seg, n):
    return jax.ops.segment_sum(src, seg, n)
kernel_name = 'mk_early_fusion_d1_tok_img512_r4_14a21c'

def setup_inputs(seed: int=0):
    np.random.seed(seed)
    _w = jnp.asarray

    def _rec_inputs():
        import jax
        import jax.numpy as jnp
        _rk = jax.random.key(seed)
        x = -0.000477451 + 1.00034 * jax.random.normal(jax.random.fold_in(_rk, 1), (16, 32, 32, 29), jnp.float32)
        txt = 0.228173 + 0.721734 * jax.random.normal(jax.random.fold_in(_rk, 2), (16, 128, 128), jnp.float32)
        return (x, txt)
    x, txt = _rec_inputs()

    def _L0_tok_setup():
        import jax, jax.numpy as jnp
        import numpy as np
        import math
        H, W_DIM, D_MODEL, B = (32, 32, 128, 128)
        F_TOTAL = 29
        SEQ_LEN = H * W_DIM

        def make_pe(seq_len: int, d_model: int) -> jnp.ndarray:
            position = np.arange(seq_len, dtype=np.float32)[:, None]
            div_term = np.exp(np.arange(0, d_model, 2, dtype=np.float32) * (-math.log(10000.0) / d_model))
            pe = np.zeros((seq_len, d_model), dtype=np.float32)
            pe[:, 0::2] = np.sin(position * div_term)
            pe[:, 1::2] = np.cos(position * div_term)
            return jnp.asarray(pe)
        key = jax.random.key(seed)
        k1, k2 = jax.random.split(key)
        state_tensor = jax.random.normal(k1, (B, H, W_DIM, F_TOTAL), dtype=jnp.float32)
        W = jax.random.normal(k2, (F_TOTAL, D_MODEL), dtype=jnp.float32) * 0.05
        return {'state_tensor': state_tensor, 'W': W}
    _L0_tok_all = _L0_tok_setup()
    _L0_tok_in = {k: v for k, v in _L0_tok_all.items() if k in ('W',)}
    del _L0_tok_all

    def _L0_attn_setup():
        import jax, jax.numpy as jnp
        import numpy as np
        D_MODEL = 128
        N_LAYERS = 2
        D_STATE = 16
        D_CONV = 4
        EXPAND = 2
        D_INNER = EXPAND * D_MODEL
        DT_RANK = (D_MODEL + 15) // 16
        B, L = (4, 256)
        LN_EPS = 1e-05

        def _layernorm(h, g, b):
            m = jnp.mean(h, axis=-1, keepdims=True)
            v = jnp.mean(jnp.square(h - m), axis=-1, keepdims=True)
            return (h - m) * jax.lax.rsqrt(v + LN_EPS) * g + b

        def _mamba_block(h, Wi, cw, cb, Wx, Wdt, bdt, A_log, Dsk, Wo):
            xz = h @ Wi
            xin, z = jnp.split(xz, 2, axis=-1)
            xc = jnp.transpose(xin, (0, 2, 1))
            xc = jnp.pad(xc, ((0, 0), (0, 0), (D_CONV - 1, 0)))
            xc = jax.lax.conv_general_dilated(xc, cw, (1,), 'VALID', dimension_numbers=('NCH', 'OIH', 'NCH'), feature_group_count=D_INNER)
            xs = jax.nn.silu(jnp.transpose(xc, (0, 2, 1)) + cb)
            dbc = xs @ Wx
            dt = dbc[..., :DT_RANK]
            Bc = dbc[..., DT_RANK:DT_RANK + D_STATE]
            Cc = dbc[..., DT_RANK + D_STATE:]
            delta = jax.nn.softplus(dt @ Wdt + bdt)
            A = -jnp.exp(A_log)
            dA = jnp.exp(delta[..., None] * A)
            dBu = (delta * xs)[..., None] * Bc[:, :, None, :]

            def step(hs, inp):
                dA_t, dBu_t, C_t = inp
                hs = dA_t * hs + dBu_t
                return (hs, jnp.einsum('bdn,bn->bd', hs, C_t))
            h0 = jnp.zeros((xs.shape[0], D_INNER, D_STATE), xs.dtype)
            _, ys = jax.lax.scan(step, h0, (jnp.transpose(dA, (1, 0, 2, 3)), jnp.transpose(dBu, (1, 0, 2, 3)), jnp.transpose(Cc, (1, 0, 2))))
            y = jnp.transpose(ys, (1, 0, 2)) + xs * Dsk
            return y * jax.nn.silu(z) @ Wo
        key = jax.random.key(seed)
        ks = jax.random.split(key, 8)
        s = 0.02
        x = jax.random.normal(ks[0], (B, L, D_MODEL), jnp.float32)
        in_proj_w = jax.random.normal(ks[1], (N_LAYERS, D_MODEL, 2 * D_INNER), jnp.float32) * s
        conv_w = jax.random.normal(ks[2], (N_LAYERS, D_INNER, 1, D_CONV), jnp.float32) * 0.1
        conv_b = jnp.zeros((N_LAYERS, D_INNER), jnp.float32)
        x_proj_w = jax.random.normal(ks[3], (N_LAYERS, D_INNER, DT_RANK + 2 * D_STATE), jnp.float32) * s
        dt_proj_w = jax.random.normal(ks[4], (N_LAYERS, DT_RANK, D_INNER), jnp.float32) * DT_RANK ** (-0.5)
        dt_proj_b = jnp.full((N_LAYERS, D_INNER), float(np.log(np.expm1(0.01))), jnp.float32)
        A_log = jnp.log(jnp.tile(jnp.arange(1, D_STATE + 1, dtype=jnp.float32), (N_LAYERS, D_INNER, 1)))
        D_skip = jnp.ones((N_LAYERS, D_INNER), jnp.float32)
        out_proj_w = jax.random.normal(ks[5], (N_LAYERS, D_INNER, D_MODEL), jnp.float32) * s
        ln_g = jnp.ones((N_LAYERS, D_MODEL), jnp.float32)
        ln_b = jnp.zeros((N_LAYERS, D_MODEL), jnp.float32)
        return {'x': x, 'in_proj_w': in_proj_w, 'conv_w': conv_w, 'conv_b': conv_b, 'x_proj_w': x_proj_w, 'dt_proj_w': dt_proj_w, 'dt_proj_b': dt_proj_b, 'A_log': A_log, 'D_skip': D_skip, 'out_proj_w': out_proj_w, 'ln_g': ln_g, 'ln_b': ln_b}
    _L0_attn_all = _L0_attn_setup()
    _L0_attn_in = {k: v for k, v in _L0_attn_all.items() if k in ('in_proj_w', 'conv_w', 'conv_b', 'x_proj_w', 'dt_proj_w', 'dt_proj_b', 'A_log', 'D_skip', 'out_proj_w', 'ln_g', 'ln_b')}
    del _L0_attn_all

    def _L0_ffn_setup():
        import jax, jax.numpy as jnp
        import numpy as np
        D = 128
        H = 8
        K = 4
        HD = D // H

        def _ln(x, w, b, eps=1e-05):
            m = x.mean(-1, keepdims=True)
            v = ((x - m) ** 2).mean(-1, keepdims=True)
            return (x - m) / jnp.sqrt(v + eps) * w + b

        def _spatial_experts(xn, idx, in_w, in_b, out_w, out_b):
            W = in_w[idx]
            qkv = jnp.einsum('btd,bed->bte', xn, W) + in_b[idx][:, None, :]
            q, k, v = jnp.split(qkv, 3, axis=-1)
            B, T, _ = xn.shape
            q = q.reshape(B, T, H, HD) * HD ** (-0.5)
            k = k.reshape(B, T, H, HD)
            v = v.reshape(B, T, H, HD)
            att = jax.nn.softmax(jnp.einsum('bthd,bshd->bhts', q, k), axis=-1)
            o = jnp.einsum('bhts,bshd->bthd', att, v).reshape(B, T, D)
            return jnp.einsum('btd,bod->bto', o, out_w[idx]) + out_b[idx][:, None, :]

        def _temporal_experts(xt, idx, qw, qb, kw, kb, vw, vb, pw, pb):
            B, T, _ = xt.shape
            q = (jnp.einsum('btd,bod->bto', xt, qw[idx]) + qb[idx][:, None, :]).reshape(B, T, H, HD)
            k = (jnp.einsum('btd,bod->bto', xt, kw[idx]) + kb[idx][:, None, :]).reshape(B, T, H, HD)
            v = (jnp.einsum('btd,bod->bto', xt, vw[idx]) + vb[idx][:, None, :]).reshape(B, T, H, HD)
            logits = jnp.einsum('bthd,bshd->bhts', q, k) * HD ** (-0.5)
            causal = jnp.tril(jnp.ones((T, T), dtype=bool))
            logits = jnp.where(causal, logits, -jnp.inf)
            att = jax.nn.softmax(logits, axis=-1)
            o = jnp.einsum('bhts,bshd->bthd', att, v).reshape(B, T, D)
            o = jnp.einsum('btd,bod->bto', o, pw[idx]) + pb[idx][:, None, :]
            return xt + o

        def _cross_mha(q_in, kv_in, in_w, in_b, out_w, out_b):
            B, T, _ = q_in.shape
            S = kv_in.shape[1]
            Wq, Wk, Wv = (in_w[:D], in_w[D:2 * D], in_w[2 * D:])
            bq, bk, bv = (in_b[:D], in_b[D:2 * D], in_b[2 * D:])
            q = (q_in @ Wq.T + bq).reshape(B, T, H, HD) * HD ** (-0.5)
            k = (kv_in @ Wk.T + bk).reshape(B, S, H, HD)
            v = (kv_in @ Wv.T + bv).reshape(B, S, H, HD)
            att = jax.nn.softmax(jnp.einsum('bthd,bshd->bhts', q, k), axis=-1)
            o = jnp.einsum('bhts,bshd->bthd', att, v).reshape(B, T, D)
            return o @ out_w.T + out_b
        key = jax.random.key(seed)
        ks = iter(jax.random.split(key, 40))
        B, T = (64, 64)
        p = lambda *shape: jax.random.normal(next(ks), shape, dtype=jnp.float32) * 0.02
        inp = {'x': jax.random.normal(next(ks), (B, T, D), dtype=jnp.float32), 'router_w1': p(128, D), 'router_b1': jnp.zeros((128,), jnp.float32), 'router_w2': p(2 * K, 128), 'router_b2': jnp.zeros((2 * K,), jnp.float32), 'norm_s_w': jnp.ones((D,), jnp.float32), 'norm_s_b': jnp.zeros((D,), jnp.float32), 'norm_t_w': jnp.ones((D,), jnp.float32), 'norm_t_b': jnp.zeros((D,), jnp.float32), 'sp_in_w': p(K, 3 * D, D), 'sp_in_b': jnp.zeros((K, 3 * D), jnp.float32), 'sp_out_w': p(K, D, D), 'sp_out_b': jnp.zeros((K, D), jnp.float32), 'tq_w': p(K, D, D), 'tq_b': jnp.zeros((K, D), jnp.float32), 'tk_w': p(K, D, D), 'tk_b': jnp.zeros((K, D), jnp.float32), 'tv_w': p(K, D, D), 'tv_b': jnp.zeros((K, D), jnp.float32), 'tp_w': p(K, D, D), 'tp_b': jnp.zeros((K, D), jnp.float32), 'cross_in_w': p(3 * D, D), 'cross_in_b': jnp.zeros((3 * D,), jnp.float32), 'cross_out_w': p(D, D), 'cross_out_b': jnp.zeros((D,), jnp.float32), 'norm_mlp_w': jnp.ones((D,), jnp.float32), 'norm_mlp_b': jnp.zeros((D,), jnp.float32), 'mlp_w1': p(4 * D, D), 'mlp_b1': jnp.zeros((4 * D,), jnp.float32), 'mlp_w2': p(D, 4 * D), 'mlp_b2': jnp.zeros((D,), jnp.float32)}
        return inp
    _L0_ffn_all = _L0_ffn_setup()
    _L0_ffn_in = {k: v for k, v in _L0_ffn_all.items() if k in ('router_w1', 'router_b1', 'router_w2', 'router_b2', 'norm_s_w', 'norm_s_b', 'norm_t_w', 'norm_t_b', 'sp_in_w', 'sp_in_b', 'sp_out_w', 'sp_out_b', 'tq_w', 'tq_b', 'tk_w', 'tk_b', 'tv_w', 'tv_b', 'tp_w', 'tp_b', 'cross_in_w', 'cross_in_b', 'cross_out_w', 'cross_out_b', 'norm_mlp_w', 'norm_mlp_b', 'mlp_w1', 'mlp_b1', 'mlp_w2', 'mlp_b2')}
    del _L0_ffn_all
    return {'x': x, 'txt': txt, 'L0_tok_W': _L0_tok_in['W'], 'L0_attn_in_proj_w': _L0_attn_in['in_proj_w'], 'L0_attn_conv_w': _L0_attn_in['conv_w'], 'L0_attn_conv_b': _L0_attn_in['conv_b'], 'L0_attn_x_proj_w': _L0_attn_in['x_proj_w'], 'L0_attn_dt_proj_w': _L0_attn_in['dt_proj_w'], 'L0_attn_dt_proj_b': _L0_attn_in['dt_proj_b'], 'L0_attn_A_log': _L0_attn_in['A_log'], 'L0_attn_D_skip': _L0_attn_in['D_skip'], 'L0_attn_out_proj_w': _L0_attn_in['out_proj_w'], 'L0_attn_ln_g': _L0_attn_in['ln_g'], 'L0_attn_ln_b': _L0_attn_in['ln_b'], 'L0_ffn_router_w1': _L0_ffn_in['router_w1'], 'L0_ffn_router_b1': _L0_ffn_in['router_b1'], 'L0_ffn_router_w2': _L0_ffn_in['router_w2'], 'L0_ffn_router_b2': _L0_ffn_in['router_b2'], 'L0_ffn_norm_s_w': _L0_ffn_in['norm_s_w'], 'L0_ffn_norm_s_b': _L0_ffn_in['norm_s_b'], 'L0_ffn_norm_t_w': _L0_ffn_in['norm_t_w'], 'L0_ffn_norm_t_b': _L0_ffn_in['norm_t_b'], 'L0_ffn_sp_in_w': _L0_ffn_in['sp_in_w'], 'L0_ffn_sp_in_b': _L0_ffn_in['sp_in_b'], 'L0_ffn_sp_out_w': _L0_ffn_in['sp_out_w'], 'L0_ffn_sp_out_b': _L0_ffn_in['sp_out_b'], 'L0_ffn_tq_w': _L0_ffn_in['tq_w'], 'L0_ffn_tq_b': _L0_ffn_in['tq_b'], 'L0_ffn_tk_w': _L0_ffn_in['tk_w'], 'L0_ffn_tk_b': _L0_ffn_in['tk_b'], 'L0_ffn_tv_w': _L0_ffn_in['tv_w'], 'L0_ffn_tv_b': _L0_ffn_in['tv_b'], 'L0_ffn_tp_w': _L0_ffn_in['tp_w'], 'L0_ffn_tp_b': _L0_ffn_in['tp_b'], 'L0_ffn_cross_in_w': _L0_ffn_in['cross_in_w'], 'L0_ffn_cross_in_b': _L0_ffn_in['cross_in_b'], 'L0_ffn_cross_out_w': _L0_ffn_in['cross_out_w'], 'L0_ffn_cross_out_b': _L0_ffn_in['cross_out_b'], 'L0_ffn_norm_mlp_w': _L0_ffn_in['norm_mlp_w'], 'L0_ffn_norm_mlp_b': _L0_ffn_in['norm_mlp_b'], 'L0_ffn_mlp_w1': _L0_ffn_in['mlp_w1'], 'L0_ffn_mlp_b1': _L0_ffn_in['mlp_b1'], 'L0_ffn_mlp_w2': _L0_ffn_in['mlp_w2'], 'L0_ffn_mlp_b2': _L0_ffn_in['mlp_b2']}

def reference(x, txt, L0_tok_W, L0_attn_in_proj_w, L0_attn_conv_w, L0_attn_conv_b, L0_attn_x_proj_w, L0_attn_dt_proj_w, L0_attn_dt_proj_b, L0_attn_A_log, L0_attn_D_skip, L0_attn_out_proj_w, L0_attn_ln_g, L0_attn_ln_b, L0_ffn_router_w1, L0_ffn_router_b1, L0_ffn_router_w2, L0_ffn_router_b2, L0_ffn_norm_s_w, L0_ffn_norm_s_b, L0_ffn_norm_t_w, L0_ffn_norm_t_b, L0_ffn_sp_in_w, L0_ffn_sp_in_b, L0_ffn_sp_out_w, L0_ffn_sp_out_b, L0_ffn_tq_w, L0_ffn_tq_b, L0_ffn_tk_w, L0_ffn_tk_b, L0_ffn_tv_w, L0_ffn_tv_b, L0_ffn_tp_w, L0_ffn_tp_b, L0_ffn_cross_in_w, L0_ffn_cross_in_b, L0_ffn_cross_out_w, L0_ffn_cross_out_b, L0_ffn_norm_mlp_w, L0_ffn_norm_mlp_b, L0_ffn_mlp_w1, L0_ffn_mlp_b1, L0_ffn_mlp_w2, L0_ffn_mlp_b2):
    import jax
    import jax.numpy as jnp

    def _L0_tok_ref(state_tensor, W):
        import jax, jax.numpy as jnp
        import numpy as np
        import math
        H, W_DIM, D_MODEL, B = (32, 32, 128, 128)
        F_TOTAL = 29
        SEQ_LEN = H * W_DIM

        def make_pe(seq_len: int, d_model: int) -> jnp.ndarray:
            position = np.arange(seq_len, dtype=np.float32)[:, None]
            div_term = np.exp(np.arange(0, d_model, 2, dtype=np.float32) * (-math.log(10000.0) / d_model))
            pe = np.zeros((seq_len, d_model), dtype=np.float32)
            pe[:, 0::2] = np.sin(position * div_term)
            pe[:, 1::2] = np.cos(position * div_term)
            return jnp.asarray(pe)
        b, h, w, f = state_tensor.shape
        s = h * w
        x = state_tensor.reshape(b, s, f)
        emb = jnp.einsum('bsf,fd->bsd', x, W)
        pe = make_pe(s * 2, W.shape[1])[:s]
        return emb + pe[None, :, :]

    def _L0_attn_ref(x, in_proj_w, conv_w, conv_b, x_proj_w, dt_proj_w, dt_proj_b, A_log, D_skip, out_proj_w, ln_g, ln_b):
        import jax, jax.numpy as jnp
        import numpy as np
        D_MODEL = 128
        N_LAYERS = 2
        D_STATE = 16
        D_CONV = 4
        EXPAND = 2
        D_INNER = EXPAND * D_MODEL
        DT_RANK = (D_MODEL + 15) // 16
        B, L = (4, 256)
        LN_EPS = 1e-05

        def _layernorm(h, g, b):
            m = jnp.mean(h, axis=-1, keepdims=True)
            v = jnp.mean(jnp.square(h - m), axis=-1, keepdims=True)
            return (h - m) * jax.lax.rsqrt(v + LN_EPS) * g + b

        def _mamba_block(h, Wi, cw, cb, Wx, Wdt, bdt, A_log, Dsk, Wo):
            xz = h @ Wi
            xin, z = jnp.split(xz, 2, axis=-1)
            xc = jnp.transpose(xin, (0, 2, 1))
            xc = jnp.pad(xc, ((0, 0), (0, 0), (D_CONV - 1, 0)))
            xc = jax.lax.conv_general_dilated(xc, cw, (1,), 'VALID', dimension_numbers=('NCH', 'OIH', 'NCH'), feature_group_count=D_INNER)
            xs = jax.nn.silu(jnp.transpose(xc, (0, 2, 1)) + cb)
            dbc = xs @ Wx
            dt = dbc[..., :DT_RANK]
            Bc = dbc[..., DT_RANK:DT_RANK + D_STATE]
            Cc = dbc[..., DT_RANK + D_STATE:]
            delta = jax.nn.softplus(dt @ Wdt + bdt)
            A = -jnp.exp(A_log)
            dA = jnp.exp(delta[..., None] * A)
            dBu = (delta * xs)[..., None] * Bc[:, :, None, :]

            def step(hs, inp):
                dA_t, dBu_t, C_t = inp
                hs = dA_t * hs + dBu_t
                return (hs, jnp.einsum('bdn,bn->bd', hs, C_t))
            h0 = jnp.zeros((xs.shape[0], D_INNER, D_STATE), xs.dtype)
            _, ys = jax.lax.scan(step, h0, (jnp.transpose(dA, (1, 0, 2, 3)), jnp.transpose(dBu, (1, 0, 2, 3)), jnp.transpose(Cc, (1, 0, 2))))
            y = jnp.transpose(ys, (1, 0, 2)) + xs * Dsk
            return y * jax.nn.silu(z) @ Wo
        h = x
        for l in range(N_LAYERS):
            h = _layernorm(_mamba_block(h, in_proj_w[l], conv_w[l], conv_b[l], x_proj_w[l], dt_proj_w[l], dt_proj_b[l], A_log[l], D_skip[l], out_proj_w[l]) + h, ln_g[l], ln_b[l])
        return h

    def _L0_ffn_ref(x, router_w1, router_b1, router_w2, router_b2, norm_s_w, norm_s_b, norm_t_w, norm_t_b, sp_in_w, sp_in_b, sp_out_w, sp_out_b, tq_w, tq_b, tk_w, tk_b, tv_w, tv_b, tp_w, tp_b, cross_in_w, cross_in_b, cross_out_w, cross_out_b, norm_mlp_w, norm_mlp_b, mlp_w1, mlp_b1, mlp_w2, mlp_b2):
        import jax, jax.numpy as jnp
        import numpy as np
        D = 128
        H = 8
        K = 4
        HD = D // H

        def _ln(x, w, b, eps=1e-05):
            m = x.mean(-1, keepdims=True)
            v = ((x - m) ** 2).mean(-1, keepdims=True)
            return (x - m) / jnp.sqrt(v + eps) * w + b

        def _spatial_experts(xn, idx, in_w, in_b, out_w, out_b):
            W = in_w[idx]
            qkv = jnp.einsum('btd,bed->bte', xn, W) + in_b[idx][:, None, :]
            q, k, v = jnp.split(qkv, 3, axis=-1)
            B, T, _ = xn.shape
            q = q.reshape(B, T, H, HD) * HD ** (-0.5)
            k = k.reshape(B, T, H, HD)
            v = v.reshape(B, T, H, HD)
            att = jax.nn.softmax(jnp.einsum('bthd,bshd->bhts', q, k), axis=-1)
            o = jnp.einsum('bhts,bshd->bthd', att, v).reshape(B, T, D)
            return jnp.einsum('btd,bod->bto', o, out_w[idx]) + out_b[idx][:, None, :]

        def _temporal_experts(xt, idx, qw, qb, kw, kb, vw, vb, pw, pb):
            B, T, _ = xt.shape
            q = (jnp.einsum('btd,bod->bto', xt, qw[idx]) + qb[idx][:, None, :]).reshape(B, T, H, HD)
            k = (jnp.einsum('btd,bod->bto', xt, kw[idx]) + kb[idx][:, None, :]).reshape(B, T, H, HD)
            v = (jnp.einsum('btd,bod->bto', xt, vw[idx]) + vb[idx][:, None, :]).reshape(B, T, H, HD)
            logits = jnp.einsum('bthd,bshd->bhts', q, k) * HD ** (-0.5)
            causal = jnp.tril(jnp.ones((T, T), dtype=bool))
            logits = jnp.where(causal, logits, -jnp.inf)
            att = jax.nn.softmax(logits, axis=-1)
            o = jnp.einsum('bhts,bshd->bthd', att, v).reshape(B, T, D)
            o = jnp.einsum('btd,bod->bto', o, pw[idx]) + pb[idx][:, None, :]
            return xt + o

        def _cross_mha(q_in, kv_in, in_w, in_b, out_w, out_b):
            B, T, _ = q_in.shape
            S = kv_in.shape[1]
            Wq, Wk, Wv = (in_w[:D], in_w[D:2 * D], in_w[2 * D:])
            bq, bk, bv = (in_b[:D], in_b[D:2 * D], in_b[2 * D:])
            q = (q_in @ Wq.T + bq).reshape(B, T, H, HD) * HD ** (-0.5)
            k = (kv_in @ Wk.T + bk).reshape(B, S, H, HD)
            v = (kv_in @ Wv.T + bv).reshape(B, S, H, HD)
            att = jax.nn.softmax(jnp.einsum('bthd,bshd->bhts', q, k), axis=-1)
            o = jnp.einsum('bhts,bshd->bthd', att, v).reshape(B, T, D)
            return o @ out_w.T + out_b
        pooled = x.mean(axis=1)
        h = jax.nn.gelu(pooled @ router_w1.T + router_b1, approximate=False)
        route = jax.nn.softmax(h @ router_w2.T + router_b2, axis=-1)
        idx_s = jnp.argmax(route[:, :K], axis=-1)
        idx_t = jnp.argmax(route[:, K:], axis=-1)
        xn = _ln(x, norm_s_w, norm_s_b)
        spatial_out = _spatial_experts(xn, idx_s, sp_in_w, sp_in_b, sp_out_w, sp_out_b)
        xt = _ln(x, norm_t_w, norm_t_b)
        temporal_out = _temporal_experts(xt, idx_t, tq_w, tq_b, tk_w, tk_b, tv_w, tv_b, tp_w, tp_b)
        fused = _cross_mha(spatial_out, temporal_out, cross_in_w, cross_in_b, cross_out_w, cross_out_b)
        x = x + fused
        h2 = _ln(x, norm_mlp_w, norm_mlp_b)
        x = x + (jax.nn.gelu(h2 @ mlp_w1.T + mlp_b1, approximate=False) @ mlp_w2.T + mlp_b2)
        return x
    h = _L0_tok_ref(x, L0_tok_W)
    h = jnp.concatenate([h, txt], axis=1)
    h = h + _L0_attn_ref(_layernorm(h, axis=-1), L0_attn_in_proj_w, L0_attn_conv_w, L0_attn_conv_b, L0_attn_x_proj_w, L0_attn_dt_proj_w, L0_attn_dt_proj_b, L0_attn_A_log, L0_attn_D_skip, L0_attn_out_proj_w, L0_attn_ln_g, L0_attn_ln_b)
    h = h + _L0_ffn_ref(_layernorm(h, axis=-1), L0_ffn_router_w1, L0_ffn_router_b1, L0_ffn_router_w2, L0_ffn_router_b2, L0_ffn_norm_s_w, L0_ffn_norm_s_b, L0_ffn_norm_t_w, L0_ffn_norm_t_b, L0_ffn_sp_in_w, L0_ffn_sp_in_b, L0_ffn_sp_out_w, L0_ffn_sp_out_b, L0_ffn_tq_w, L0_ffn_tq_b, L0_ffn_tk_w, L0_ffn_tk_b, L0_ffn_tv_w, L0_ffn_tv_b, L0_ffn_tp_w, L0_ffn_tp_b, L0_ffn_cross_in_w, L0_ffn_cross_in_b, L0_ffn_cross_out_w, L0_ffn_cross_out_b, L0_ffn_norm_mlp_w, L0_ffn_norm_mlp_b, L0_ffn_mlp_w1, L0_ffn_mlp_b1, L0_ffn_mlp_w2, L0_ffn_mlp_b2)
    return h

_drawn_inputs = setup_inputs


def setup_inputs(seed=0):
    import zlib

    import numpy as np

    out = dict(_drawn_inputs(seed))
    spreads = {'L0_attn_conv_b': (0.0, 0.8),
     'L0_attn_dt_proj_b': (-4.600165843963623, 0.6),
     'L0_attn_D_skip': (1.0, 0.6),
     'L0_attn_ln_g': (1.0, 0.2),
     'L0_attn_ln_b': (0.0, 0.1),
     'L0_ffn_router_b1': (0.0, 0.1),
     'L0_ffn_router_b2': (0.0, 0.8),
     'L0_ffn_norm_s_w': (1.0, 0.6),
     'L0_ffn_norm_s_b': (0.0, 0.8),
     'L0_ffn_norm_t_w': (1.0, 0.6),
     'L0_ffn_norm_t_b': (0.0, 0.8),
     'L0_ffn_sp_in_b': (0.0, 0.8),
     'L0_ffn_sp_out_b': (0.0, 0.8),
     'L0_ffn_tq_b': (0.0, 0.8),
     'L0_ffn_tk_b': (0.0, 2.0),
     'L0_ffn_tv_b': (0.0, 0.8),
     'L0_ffn_tp_b': (0.0, 0.8),
     'L0_ffn_cross_in_b': (0.0, 0.8),
     'L0_ffn_cross_out_b': (0.0, 0.7),
     'L0_ffn_norm_mlp_w': (1.0, 0.6),
     'L0_ffn_norm_mlp_b': (0.0, 2.0),
     'L0_ffn_mlp_b1': (0.0, 0.8),
     'L0_ffn_mlp_b2': (0.0, 0.668)}
    factors = {'L0_attn_in_proj_w': 8.0,
     'L0_attn_conv_w': 8.0,
     'L0_attn_x_proj_w': 8.0,
     'L0_attn_dt_proj_w': 8.0,
     'L0_attn_A_log': 8.0,
     'L0_attn_out_proj_w': 8.0,
     'L0_ffn_router_w1': 8.0,
     'L0_ffn_router_w2': 8.0,
     'L0_ffn_sp_in_w': 8.0,
     'L0_ffn_sp_out_w': 8.0,
     'L0_ffn_tq_w': 8.0,
     'L0_ffn_tk_w': 8.0,
     'L0_ffn_tv_w': 8.0,
     'L0_ffn_tp_w': 8.0,
     'L0_ffn_cross_in_w': 6.505,
     'L0_ffn_cross_out_w': 4.652,
     'L0_ffn_mlp_w1': 2.789}
    for name, (base, spread) in spreads.items():
        noise = np.random.default_rng([zlib.crc32(name.encode()), seed]).standard_normal(out[name].shape)
        drawn = base * np.exp(spread * noise) if base else spread * noise
        out[name] = jnp.asarray(drawn.astype(out[name].dtype))
    for name, factor in factors.items():
        out[name] = (out[name] * factor).astype(out[name].dtype)
    return out
```

```python
import math

import numpy as np

import concourse.bass as bass
from concourse import mybir
from contextlib import ExitStack

P = 128
TXT, IMG = 128, 1024
T = TXT + IMG
D = 128
FEAT = 29
L = 2
TAPS, NS, RANK = 4, 16, 8
U = 2
HEADS, HD = 8, 16
EXP = 4
NB = T // P
C3 = 384
TH = T // 2
TQ = TH // 2
EPS = 1e-5
SMALL_E = 2.0 ** -10
LAG = 3
OUTS = 4
KQ = 6 * HD
SR = 3 * 32 + RANK
ATT = 3
AW = 6 * P + 3

_F32 = [
    ("tok_w", D), ("pe", IMG), ("wi", L * 512), ("conv_b", L * U),
    ("wx", L * U * SR), ("wdt", L * 256), ("bdt", L * U), ("a_log", L * U * NS), ("d_skip", L * U),
    ("wo", L * U * D), ("ln_g", L), ("ln_b", L), ("r_w1", D), ("r_b1", 1), ("r_w2", 2 * EXP),
    ("r_b2", 2 * EXP), ("norms", 6), ("expert", EXP * 2 * AW), ("cross", AW), ("m_w1", 4 * D),
    ("m_b1", 4), ("m_w2", 4 * D), ("m_b2", 1), ("mean_mat", P), ("identf", P), ("sum_row", 4),
    ("masks", 2), ("eps", 1), ("conv_w", L * TAPS * 256),
]
F32_AT = {}
_n = 0
for _name, _w in _F32:
    F32_AT[_name] = (_n, _n + _w)
    _n += _w
F32_COLS = _n
KEPT_COLS = F32_AT["conv_w"][0]
BF_COLS = 3 * P + 2 * NS * P

PER = dict(
    tokens_in=32, emb_sum=1, ln_src=5, ln_mean=6, ln_centered=6, ln_squared=6, ln_var=6, ln_std=6, ln_rstd=6, ln_bcast=6, ln_out=6,
    xc_sum=4, z_sum=4, xs_ready=4, zs_ready=4, dbc_sum=2, bc_hi=2, bc_rest=2, bc_mid=2, bc_parts=2,
    dt_rows=2, dt_sum=4, dt_abs=4, dt_read=4, dt_exp=4, dt_log=4, delta_ready=4, dx_ready=4,
    b_bcast=64, c_bcast=64, c_copied=64, decay_ready=128, input_ready=64, state_ready=128,
    out_ready=64, y_sum=64, y_read=4, gated=4, wo_sum=2,
    pooled=1, r_hidden_sum=1, r_hidden=1, r_bcast=1, r_sum=1, chosen=1,
    att_in=2, q_sum=3, k_sum=3, v_sum=3, q_read=3, k_read=3, v_read=3,
    q_hi=3, q_rest=3, q_mid=3, q_parts=3, k_hi=3, k_rest=3, k_mid=3, k_parts=3,
    parts_out=3 * 32, stacks_in=3 * 12 * 16, max_rows_in=0,
    max_scores=0, max_read=0, max_split=0, max_turned=0, max_rows=0,
    scores=0, weights=0, weights_used=0, heads_read=0, denom=3, denom_inv=3, denom_bcast=6, heads_out=6, proj_sum=3, att_out=2,
    mlp_sum=4, mlp_hidden=4, mlp_out_sum=1, result=1, stored=16,
    dve_step=0, log_waited=4, last_saved=32, ones_ready=1,
)


def score_units(causal):
    return [(qc, kb) for qc in range(3) for kb in range(min(NB, 3 * qc + 3) if causal else NB)]


def max_units(causal):
    return [(j, qb, c) for j in range(2) for qb in range(NB) for c in range(qb // 3 + 1 if causal else 3)]


def attention_order(causal):
    units, tops = score_units(causal), max_units(causal)
    order = [("max", 0, i) for i in range(len(tops))] + [("split", 0), ("turn", 0), ("rows", 0)]
    for pair in range(PAIRS):
        more = [("max", pair + 1, i) for i in range(len(tops))] if pair + 1 < PAIRS else []
        rate = -(-len(tops) // (len(units) - 4))
        late = [("split", pair + 1), ("turn", pair + 1), ("rows", pair + 1)] if more else []
        for i in range(len(units) + 1):
            if i < len(units):
                order.append(("exp", pair, i))
            if more:
                order += more[:rate]
                more = more[rate:]
            elif late:
                order.append(late.pop(0))
            if i > 0:
                order.append(("weigh", pair, i - 1))
                qc, kb = units[i - 1]
                if i == len(units) or units[i][0] != qc:
                    order.append(("read", pair, qc))
        order += late
    return order


PAIRS = HEADS // 2
ORDER = [attention_order(a == 1) for a in range(ATT)]
N_SCORES = [PAIRS * len(score_units(a == 1)) for a in range(ATT)]
N_MAX = [PAIRS * len(max_units(a == 1)) for a in range(ATT)]
PER["scores"] = PER["weights"] = PER["weights_used"] = sum(N_SCORES)
PER["max_scores"] = PER["max_read"] = sum(N_MAX)
PER["heads_read"] = ATT * PAIRS * 3
PER["max_split"] = PER["max_turned"] = PER["max_rows"] = ATT * PAIRS
PER["max_rows_in"] = ATT * PAIRS * 3 * 16
PER["dve_step"] = 123


def fusion_kernel(nc, xT, txtT, params, consts, out):
    f32, bf16 = mybir.dt.float32, mybir.dt.bfloat16
    ALU = mybir.AluOpType
    ACT = mybir.ActivationFunctionType
    AX = mybir.AxisListType
    B = xT.shape[0]
    ctx = ExitStack()
    with ctx:
        def sb(name, shape, dt=f32):
            return ctx.enter_context(nc.sbuf_tensor(name, shape, dt))

        S = {name: ctx.enter_context(nc.semaphore(name)) for name in PER}
        loaded = ctx.enter_context(nc.semaphore("loaded"))
        convs_ready = ctx.enter_context(nc.semaphore("convs_ready"))
        decays_ready = ctx.enter_context(nc.semaphore("decays_ready"))
        turns = ctx.enter_context(nc.semaphore("turns"))

        W = sb("W", [P, KEPT_COLS])
        CB = sb("CB", [P, BF_COLS], bf16)
        conv_wi = sb("conv_wi", [P, L, TAPS, 256])
        a_neg = sb("a_neg", [P, L * U * NS])
        h_pad = sb("h_pad", [P, 3 + T])
        h0 = sb("h0", [P, T])
        res = sb("res", [P, T])
        cen = sb("cen", [P, T])
        sq = sb("sq", [P, T])
        rstd = sb("rstd", [P, T])
        result = sb("result_sb", [P, T])
        stats = sb("stats", [P, 4 * NB])
        deviation = stats[:, 3 * NB:4 * NB]
        ARENA = 28200
        arena = sb("arena", [P, ARENA])
        at = [0]

        def part(n):
            at[0] += n
            assert at[0] <= ARENA, at
            return arena[:, at[0] - n:at[0]]

        xs = part(U * T).rearrange("p (u t) -> p u t", u=U)
        zs = part(U * T).rearrange("p (u t) -> p u t", u=U)
        delta = part(U * T).rearrange("p (u t) -> p u t", u=U)
        dx = part(U * T).rearrange("p (u t) -> p u t", u=U)
        gate = part(U * T).rearrange("p (u t) -> p u t", u=U)
        bc_rest = part(T)
        bc_hi = cen[:, 0:T // 2].bitcast(bf16)
        bc_mid = cen[:, T // 2:T].bitcast(bf16)
        bc_parts = part(T // 2).bitcast(bf16)
        dt_rows = bc_rest
        e_small = result[:, 0:T // 4].bitcast(mybir.dt.uint8)
        decay = part(2 * U * TH).rearrange("p (r u t) -> p r u t", r=2, u=U)
        drive = [buf[:, :].rearrange("p (u t) -> p u t", u=U) for buf in (sq, rstd, cen)]
        state = part(3 * U * TH).rearrange("p (r u t) -> p r u t", r=3, u=U)
        outs = part(OUTS * U * TH).rearrange("p (r u t) -> p r u t", r=OUTS, u=U)
        c_sb = part(3 * TH).rearrange("p (r t) -> p r t", r=3)
        last = part(U * NS).rearrange("p (u n) -> p u n", u=U)
        at[0] = 0
        q_stack = part(HEADS * T // 2).bitcast(bf16).rearrange("p (h t) -> p h t", h=HEADS)
        k_stack = part(HEADS * T // 2).bitcast(bf16).rearrange("p (h t) -> p h t", h=HEADS)
        v_aug = part(NB * HEADS * 32).rearrange("p (k h c) -> p k h c", k=NB, h=HEADS)
        q_parts = part(3 * T // 2).bitcast(bf16).rearrange("p (s t) -> p s t", s=3)
        k_parts = part(3 * T // 2).bitcast(bf16).rearrange("p (s t) -> p s t", s=3)
        wts = part(3 * 2 * C3).rearrange("p (r i t) -> p r i t", r=3, i=2)
        inverse_rows = arena[:, at[0] - 3 * 2 * C3:at[0]]
        heads_o = part(2 * T).rearrange("p (g t) -> p g t", g=2)
        xhat = part(T)
        s_out = part(T)
        t_in = part(T)
        t_out = part(T)
        qf = part(T)
        chosen = part(2 * AW)
        hidden_bc = part(P)
        small = part(64)
        inverse = part(8 * NB)
        max3 = part(NB * HEADS * 3).rearrange("p (r k h c) -> p r k h c", r=4, k=NB, h=2)
        neg_max = part(NB * HEADS).rearrange("p (r k h) -> p r k h", r=4, k=NB)
        max_tmp = part(NB * HEADS).rearrange("p (r k h) -> p r k h", r=4, k=NB)
        max_parts = part(3 * NB * HEADS // 2).bitcast(bf16).rearrange("p (r k s h) -> p r k s h", r=4, k=NB, s=3)
        max_rows = part(T // 2).bitcast(bf16)
        hidden = arena[:, 0:4 * T].rearrange("p (m t) -> p m t", m=4)

        PS = ctx.enter_context(nc.psum_tensor("PS", [P, 8, 512], f32))

        def slot(n, rows=P):
            return PS[0:rows, 3 * n:3 * n + 3, 0:C3]

        def banks3(ap):
            return ap.rearrange("p (c t) -> p c t", c=3)

        parts_dram = nc.dram_tensor("parts_dram", (2, P, 3, T), bf16, kind="Internal")

        def w(name):
            a, z = F32_AT[name]
            return W[:, a:z]

        tok_w = w("tok_w")[0:FEAT, :]
        wi = w("wi").rearrange("p (l n) -> p l n", l=L)
        consts_f32 = arena[:, L * TAPS * 256:L * TAPS * 256 + BF_COLS]
        conv_w = arena[:, 0:L * TAPS * 256].rearrange("p (l j n) -> p l j n", l=L, j=TAPS)
        wx = w("wx").rearrange("p (l u n) -> p l u n", l=L, u=U)
        wdt = w("wdt").rearrange("p (l n) -> p l n", l=L)
        wo = w("wo").rearrange("p (l u n) -> p l u n", l=L, u=U)
        norms = w("norms")
        expert = w("expert").rearrange("p (e a) -> p e a", e=EXP)
        cross = w("cross")
        mean_mat, identf, sum_row, masks = w("mean_mat"), w("identf"), w("sum_row"), w("masks")
        ident, mask_q, mask_k = CB[:, 0:P], CB[:, P:2 * P], CB[:, 2 * P:3 * P]
        pick = CB[0:96, 3 * P:].rearrange("p (n m) -> p n m", n=2 * NS)

        def aw(a, what):
            base = cross if a == 2 else chosen[:, a * AW:(a + 1) * AW]
            cols = dict(q=(0, P), k=(P, 2 * P), v=(2 * P, 3 * P), vb=(3 * P, 4 * P), o0=(4 * P, 5 * P),
                        o1=(5 * P, 6 * P), qb=(6 * P, 6 * P + 1), kb=(6 * P + 1, 6 * P + 2),
                        ob=(6 * P + 2, 6 * P + 3))[what]
            return base[:, cols[0]:cols[1]]

        def att_q(a):
            return [xhat, t_in, s_out][a]

        def att_kv(a):
            return [xhat, t_in, t_out][a]

        block = ctx.enter_context(nc.Block())

        @block.sync
        def _(sp):
            sp.dma_start(W[:, :], params[:, 0:KEPT_COLS]).then_inc(loaded, 16)
            sp.dma_start(arena[:, 0:L * TAPS * 256], params[:, KEPT_COLS:F32_COLS]).then_inc(loaded, 16)
            sp.dma_start(consts_f32, consts).then_inc(loaded, 16)
            with sp.Fori(0, B) as b:
                sp.dma_start(cen[0:FEAT, 0:IMG], xT[bass.ds(b, 1), :, :].rearrange("o f t -> (o f) t")).then_inc(S["tokens_in"], 16)
                sp.dma_start(h0[:, IMG:T], txtT[bass.ds(b, 1), :, :].rearrange("o f t -> (o f) t")).then_inc(S["tokens_in"], 16)
                for a in range(ATT):
                    sp.wait_ge(S["k_parts"], b * PER["k_parts"] + a + 1)
                    sp.dma_start(parts_dram[1, :, :, :], k_parts).then_inc(S["parts_out"], 16)
                    sp.wait_ge(S["q_parts"], b * PER["q_parts"] + a + 1)
                    sp.dma_start(parts_dram[0, :, :, :], q_parts).then_inc(S["parts_out"], 16)
                    sp.wait_ge(S["parts_out"], b * PER["parts_out"] + 32 * (a + 1))
                    for j in range(6):
                        qp, kp = (0, 0, 1, 1, 0, 2)[j], (0, 1, 0, 1, 2, 0)[j]
                        for n, s, dst in ((0, qp, q_stack), (1, kp, k_stack)):
                            src = parts_dram[n, :, s, :].rearrange("(h d) t -> d h t", h=HEADS)
                            sp.dma_start(dst[HD * j:HD * (j + 1), :, :], src).then_inc(S["stacks_in"], 16)
                    for pair in range(PAIRS):
                        sp.wait_ge(S["max_rows"], b * PER["max_rows"] + PAIRS * a + pair + 1)
                        for s in range(3):
                            sp.dma_start(q_stack[KQ + s:KQ + s + 1, 2 * pair:2 * pair + 2, :],
                                            max_rows[2 * s:2 * s + 2, :]).then_inc(S["max_rows_in"], 16)
                sp.wait_ge(S["result"], b * PER["result"] + 1)
                sp.dma_start(out[bass.ds(b, 1), :, :].rearrange("o f t -> (o f) t"), result[:, :]).then_inc(S["stored"], 16)
                sp.wait_ge(S["stored"], b * PER["stored"] + 16)
                sp.sem_inc(turns, 1)
            sp.wait_ge(S["stored"], 16 * B)

        @block.tensor
        def _(pe):
            mm = nc.tensor.matmul
            pe.wait_ge(loaded, 48)
            pe.wait_ge(convs_ready, 1)

            def dense(n, pairs, rows=P):
                for c in range(3):
                    for i, (lhsT, rhs) in enumerate(pairs):
                        x = mm(PS[0:rows, 3 * n + c, 0:C3], lhsT, rhs[:, c * C3:(c + 1) * C3],
                               start=(i == 0), stop=(i == len(pairs) - 1))
                return x

            with pe.Fori(0, B) as b:
                def layer_norm(i, src, ready, k):
                    pe.wait_ge(S[ready], b * PER[ready] + k)
                    dense(0, [(mean_mat, src)]).then_inc(S["ln_mean"], 1)
                    pe.wait_ge(S["ln_squared"], b * PER["ln_squared"] + i + 1)
                    for k in range(NB):
                        x = mm(PS[:, 6, k:k + 1], sq[:, k * P:(k + 1) * P], mean_mat[:, 0:1], start=True, stop=True)
                    x.then_inc(S["ln_var"], 1)
                    pe.wait_ge(S["ln_rstd"], b * PER["ln_rstd"] + i + 1)
                    for k in range(NB):
                        x = mm(PS[:, 3 + k // 3, (k % 3) * P:(k % 3 + 1) * P], stats[:, k:k + 1].broadcast_to([P, P]),
                               identf, start=True, stop=True)
                    x.then_inc(S["ln_bcast"], 1)

                pe.wait_ge(S["tokens_in"], b * PER["tokens_in"] + 32)
                for c, (s, e) in enumerate(((0, C3), (C3, 2 * C3), (2 * C3, IMG))):
                    x = mm(PS[:, c, 0:e - s], tok_w, cen[0:FEAT, s:e], start=True, stop=True)
                x.then_inc(S["emb_sum"], 1)
                layer_norm(0, h0, "ln_src", 1)

                for l in range(L):
                    pe.wait_ge(S["ln_out"], b * PER["ln_out"] + l + 1)
                    for u in range(U):
                        dense(u, [(conv_wi[:, l, j, u * P:(u + 1) * P], h_pad[:, j:j + T])
                                     for j in range(TAPS)]).then_inc(S["xc_sum"], 1)
                    pe.wait_ge(S["xs_ready"], b * PER["xs_ready"] + 2 * l + 2)
                    dense(0, [(wx[:, l, u, :], xs[:, u, :]) for u in range(U)], SR).then_inc(S["dbc_sum"], 1)
                    dense(1, [(wi[:, l, 256:256 + P], h_pad[:, 3:3 + T])]).then_inc(S["z_sum"], 1)
                    pe.wait_ge(S["dt_rows"], b * PER["dt_rows"] + l + 1)
                    pe.wait_ge(S["zs_ready"], b * PER["zs_ready"] + 2 * l + 1)
                    for u in range(U):
                        if u == 1:
                            pe.wait_ge(S["bc_rest"], b * PER["bc_rest"] + l + 1)
                            pe.wait_ge(S["bc_hi"], b * PER["bc_hi"] + l + 1)
                        dense(1 - u, [(wdt[96:96 + RANK, l, u * P:(u + 1) * P], dt_rows[96:96 + RANK, :])]).then_inc(S["dt_sum"], 1)
                    pe.wait_ge(S["dt_read"], b * PER["dt_read"] + 2 * l + 1)
                    dense(1, [(wi[:, l, 256 + P:512], h_pad[:, 3:3 + T])]).then_inc(S["z_sum"], 1)
                    pe.wait_ge(S["bc_parts"], b * PER["bc_parts"] + l + 1)
                    pe.wait_ge(S["dt_read"], b * PER["dt_read"] + 2 * l + 2)
                    pe.wait_ge(S["zs_ready"], b * PER["zs_ready"] + 2 * l + 2)

                    def accumulate(r):
                        k, n = (r // NS) % 2, r % NS
                        pe.wait_ge(S["out_ready"], b * PER["out_ready"] + r + 1)
                        if n == 0 and r > 0:
                            pe.wait_ge(S["y_read"], b * PER["y_read"] + r // NS)
                        for u in range(U):
                            for q in range(2):
                                x = mm(PS[:, 2 * u + q, 0:TQ], identf, outs[:, r % OUTS, u, q * TQ:(q + 1) * TQ],
                                       start=(n == 0), stop=(n == NS - 1))
                        x.then_inc(S["y_sum"], 1)

                    for r in range(32 * l, 32 * l + 32):
                        k, n = (r // NS) % 2, r % NS
                        t0 = k * TH
                        if r > 0:
                            pe.wait_ge(S["input_ready"], b * PER["input_ready"] + r)
                        for q in range(2):
                            x = mm(PS[:, 4 + q, 0:TQ], pick[:, n, :], bc_parts[0:96, t0 + q * TQ:t0 + (q + 1) * TQ],
                                   start=True, stop=True)
                        x.then_inc(S["b_bcast"], 1)
                        if r > 0:
                            pe.wait_ge(S["c_copied"], b * PER["c_copied"] + r)
                        for q in range(2):
                            x = mm(PS[:, 6 + q, 0:TQ], pick[:, NS + n, :], bc_parts[0:96, t0 + q * TQ:t0 + (q + 1) * TQ],
                                   start=True, stop=True)
                        x.then_inc(S["c_bcast"], 1)
                        if r >= 32 * l + LAG:
                            accumulate(r - LAG)
                    for r in range(32 * l + 32 - LAG, 32 * l + 32):
                        accumulate(r)
                    pe.wait_ge(S["gated"], b * PER["gated"] + 2 * l + 2)
                    pe.wait_ge(S["y_read"], b * PER["y_read"] + 2 * l + 2)
                    dense(0, [(wo[:, l, u, :], gate[:, u, :]) for u in range(U)]).then_inc(S["wo_sum"], 1)
                    layer_norm(l + 1, res, "ln_src", l + 2)

                layer_norm(3, h0, "ln_src", 4)
                pe.wait_ge(S["pooled"], b * PER["pooled"] + 1)
                mm(PS[:, 6, 0:1], w("r_w1"), small[:, 0:1], start=True, stop=True).then_inc(S["r_hidden_sum"], 1)
                pe.wait_ge(S["r_bcast"], b * PER["r_bcast"] + 1)
                mm(PS[:, 7, 0:2 * EXP], hidden_bc, w("r_w2"), start=True, stop=True).then_inc(S["r_sum"], 1)
                layer_norm(4, res, "ln_out", 4)

                for a in range(ATT):
                    if a == 0:
                        pe.wait_ge(S["chosen"], b * PER["chosen"] + 1)
                        pe.wait_ge(S["att_in"], b * PER["att_in"] + 1)
                    else:
                        pe.wait_ge(S["att_in"], b * PER["att_in"] + 2)
                        pe.wait_ge(S["att_out"], b * PER["att_out"] + a)
                    dense(0, [(aw(a, "q"), att_q(a))]).then_inc(S["q_sum"], 1)
                    dense(1, [(aw(a, "k"), att_kv(a))]).then_inc(S["k_sum"], 1)
                    pe.wait_ge(S["q_read"], b * PER["q_read"] + a + 1)
                    for k in range(NB):
                        x = mm(PS[:, k // 3, (k % 3) * P:(k % 3 + 1) * P], att_kv(a)[:, k * P:(k + 1) * P],
                               aw(a, "v"), start=True, stop=True)
                    x.then_inc(S["v_sum"], 1)

                    pe.wait_ge(S["stacks_in"], b * PER["stacks_in"] + 192 * (a + 1))
                    pe.wait_ge(S["v_read"], b * PER["v_read"] + a + 1)
                    pe.wait_ge(S["k_read"], b * PER["k_read"] + a + 1)
                    units, tops = score_units(a == 1), max_units(a == 1)
                    top0, unit0 = sum(N_MAX[:a]), sum(N_SCORES[:a])
                    for what, pair, *rest in ORDER[a]:
                        if what == "max":
                            j, qb, c = tops[rest[0]]
                            h, m = 2 * pair + j, top0 + pair * len(tops) + rest[0]
                            if m >= top0 + 3:
                                pe.wait_ge(S["max_read"], b * PER["max_read"] + m - 2)
                            cols = min(C3, P * (qb + 1) - C3 * c) if a == 1 else C3
                            diag = a == 1 and c == qb // 3
                            dst = PS[:, 5 + m % 3, 0:cols]
                            x = mm(dst, q_stack[0:KQ, h, qb * P:(qb + 1) * P],
                                   k_stack[0:KQ, h, c * C3:c * C3 + cols], start=True, stop=not diag)
                            if diag:
                                x = mm(dst[:, cols - P:cols], ident, mask_q, start=False, stop=True)
                            x.then_inc(S["max_scores"], 1)
                        elif what == "turn":
                            pe.wait_ge(S["max_split"], b * PER["max_split"] + PAIRS * a + pair + 1)
                            for k in range(NB):
                                x = mm(PS[0:6, 5 + k // 3, (k % 3) * P:(k % 3 + 1) * P],
                                       max_parts[:, pair, k, :, :].rearrange("p s h -> p (s h)"), ident,
                                       start=True, stop=True)
                            x.then_inc(S["max_turned"], 1)
                        elif what == "exp":
                            i = rest[0]
                            qc, kb = units[i]
                            n = unit0 + pair * len(units) + i
                            if i == 0:
                                pe.wait_ge(S["max_rows_in"], b * PER["max_rows_in"] + 48 * (PAIRS * a + pair + 1))
                                if a == 0 and pair == 0:
                                    pe.wait_ge(S["ones_ready"], b * PER["ones_ready"] + 1)
                            if n >= unit0 + 2:
                                pe.wait_ge(S["weights"], b * PER["weights"] + n - 1)
                            s = max(0, P * kb - C3 * qc) if a == 1 else 0
                            diag = a == 1 and kb >= 3 * qc
                            for j in range(2):
                                h, bank = 2 * pair + j, 2 * (n % 2) + j
                                x = mm(PS[:, bank, s:C3], k_stack[0:KQ + 3, h, kb * P:(kb + 1) * P],
                                       q_stack[0:KQ + 3, h, qc * C3 + s:(qc + 1) * C3], start=True, stop=not diag)
                                if diag:
                                    x = mm(PS[:, bank, s:s + P], ident, mask_k, start=False, stop=True)
                            x.then_inc(S["scores"], 1)
                        elif what == "weigh":
                            i = rest[0]
                            qc, kb = units[i]
                            n = unit0 + pair * len(units) + i
                            reads = 3 * PAIRS * a + 3 * pair + qc
                            pe.wait_ge(S["weights"], b * PER["weights"] + n + 1)
                            if kb == 0 and reads > 3 * PAIRS * a:
                                pe.wait_ge(S["heads_read"], b * PER["heads_read"] + reads)
                            s = max(0, P * kb - C3 * qc) if a == 1 else 0
                            last_kb = (min(NB, 3 * qc + 3) if a == 1 else NB) - 1
                            for j in range(2):
                                o = 64 * (pair % 2) + 32 * j
                                x = mm(PS[o:o + 32, 4, s:C3], v_aug[:, kb, 2 * pair + j, :], wts[:, n % 3, j, s:C3],
                                       start=(kb == 0), stop=(kb == last_kb))
                            x.then_inc(S["weights_used"], 1)
                    pe.wait_ge(S["heads_read"], b * PER["heads_read"] + 3 * PAIRS * (a + 1))
                    for g in range(2):
                        for k in range(NB):
                            o = 4 * (NB * g + k)
                            x = mm(PS[:, 6, o:o + 4], heads_o[:, g, k * P:(k + 1) * P], sum_row[:, 0:4],
                                   start=True, stop=True)
                    x.then_inc(S["denom"], 1)
                    pe.wait_ge(S["denom_inv"], b * PER["denom_inv"] + a + 1)
                    for g in range(2):
                        for k in range(NB):
                            o = 4 * (NB * g + k)
                            x = mm(PS[:, 3 * g + k // 3, (k % 3) * P:(k % 3 + 1) * P],
                                   inverse_rows[:, 32 * o:32 * o + P], identf, start=True, stop=True)
                        x.then_inc(S["denom_bcast"], 1)
                    pe.wait_ge(S["heads_out"], b * PER["heads_out"] + 2 * a + 2)
                    dense(0, [(aw(a, "o0"), heads_o[:, 0, :]), (aw(a, "o1"), heads_o[:, 1, :])]).then_inc(S["proj_sum"], 1)

                layer_norm(5, res, "ln_src", 5)
                pe.wait_ge(S["ln_out"], b * PER["ln_out"] + 6)
                for m in range(4):
                    if m >= 2:
                        pe.wait_ge(S["mlp_hidden"], b * PER["mlp_hidden"] + m - 1)
                    dense(m % 2, [(w("m_w1")[:, m * P:(m + 1) * P], xhat)]).then_inc(S["mlp_sum"], 1)
                pe.wait_ge(S["mlp_hidden"], b * PER["mlp_hidden"] + 4)
                dense(0, [(w("m_w2")[:, m * P:(m + 1) * P], hidden[:, m, :]) for m in range(4)]).then_inc(S["mlp_out_sum"], 1)

        @block.scalar
        def _(act):
            A = nc.scalar.activation
            act.wait_ge(loaded, 48)
            A(a_neg[:, :], w("a_log"), ACT.Exp).then_inc(decays_ready, 1)
            act.wait_ge(decays_ready, 2)
            with act.Fori(0, B) as b:
                def layer_norm(i):
                    act.wait_ge(S["ln_centered"], b * PER["ln_centered"] + i + 1)
                    A(sq[:, :], cen[:, :], ACT.Square).then_inc(S["ln_squared"], 1)
                    act.wait_ge(S["ln_var"], b * PER["ln_var"] + i + 1)
                    A(deviation, PS[:, 6, 0:NB], ACT.Sqrt, bias=w("eps")).then_inc(S["ln_std"], 1)

                layer_norm(0)
                for l in range(L):
                    def silu_z(u):
                        act.wait_ge(S["z_sum"], b * PER["z_sum"] + 2 * l + u + 1)
                        A(banks3(zs[:, u, :]), slot(1), ACT.Silu).then_inc(S["zs_ready"], 1)

                    for u in range(U):
                        act.wait_ge(S["xc_sum"], b * PER["xc_sum"] + 2 * l + u + 1)
                        A(banks3(xs[:, u, :]), slot(u), ACT.Silu, bias=w("conv_b")[:, 2 * l + u:2 * l + u + 1]).then_inc(S["xs_ready"], 1)
                    act.wait_ge(S["dbc_sum"], b * PER["dbc_sum"] + l + 1)
                    A(banks3(dt_rows[96:96 + RANK, :]), slot(0)[96:96 + RANK], ACT.Copy).then_inc(S["dt_rows"], 1)
                    A(banks3(bc_hi[0:96, :]), slot(0)[0:96], ACT.Copy).then_inc(S["bc_hi"], 1)
                    silu_z(0)
                    act.wait_ge(S["bc_rest"], b * PER["bc_rest"] + l + 1)
                    A(bc_mid[0:96, :], bc_rest[0:96, :], ACT.Copy).then_inc(S["bc_mid"], 1)
                    for u in range(U):
                        act.wait_ge(S["dt_sum"], b * PER["dt_sum"] + 2 * l + u + 1)
                        A(banks3(gate[:, u, :]), slot(1 - u), ACT.Abs, bias=w("bdt")[:, 2 * l + u:2 * l + u + 1]).then_inc(S["dt_abs"], 1)
                        act.wait_ge(S["dt_abs"], b * PER["dt_abs"] + 2 * l + u + 1)
                        A(dx[:, u, :], gate[:, u, :], ACT.Exp, scale=-1.0).then_inc(S["dt_exp"], 1)
                        act.wait_ge(S["dt_exp"], b * PER["dt_exp"] + 2 * l + u + 1)
                        A(gate[:, u, :], dx[:, u, :], ACT.Ln, bias=1.0).then_inc(S["dt_log"], 1)
                    silu_z(1)
                    act.wait_ge(S["delta_ready"], b * PER["delta_ready"] + 2 * l + 2)
                    for r in range(32 * l, 32 * l + 32):
                        k, n = (r // NS) % 2, r % NS
                        t0 = k * TH
                        if r >= 2:
                            act.wait_ge(S["state_ready"], b * PER["state_ready"] + 2 * (r - 1))
                        for u in range(U):
                            col = (l * U + u) * NS + n
                            A(decay[:, r % 2, u, :], delta[:, u, t0:t0 + TH], ACT.Exp,
                                 scale=a_neg[:, col:col + 1]).then_inc(S["decay_ready"], 1)
                        act.wait_ge(S["c_bcast"], b * PER["c_bcast"] + r + 1)
                        if r >= 3:
                            act.wait_ge(S["out_ready"], b * PER["out_ready"] + r - 2)
                        A(c_sb[:, r % 3, :].rearrange("p (q t) -> p q t", q=2), PS[:, 6:8, 0:TQ], ACT.Copy).then_inc(S["c_copied"], 1)
                    layer_norm(l + 1)
                layer_norm(3)
                act.wait_ge(S["r_hidden_sum"], b * PER["r_hidden_sum"] + 1)
                A(small[:, 1:2], PS[:, 6, 0:1], ACT.Gelu, bias=w("r_b1")).then_inc(S["r_hidden"], 1)
                layer_norm(4)
                for a in range(ATT):
                    act.wait_ge(S["k_sum"], b * PER["k_sum"] + a + 1)
                    A(banks3(qf), slot(1), ACT.Identity, bias=aw(a, "kb")).then_inc(S["k_read"], 1)
                    act.wait_ge(S["k_read"], b * PER["k_read"] + a + 1)
                    A(k_parts[:, 0, :], qf, ACT.Copy).then_inc(S["k_hi"], 1)
                    act.wait_ge(S["k_rest"], b * PER["k_rest"] + a + 1)
                    A(k_parts[:, 1, :], sq[:, :], ACT.Copy).then_inc(S["k_mid"], 1)
                    act.wait_ge(S["q_read"], b * PER["q_read"] + a + 1)
                    A(q_parts[:, 0, :], cen[:, :], ACT.Copy).then_inc(S["q_hi"], 1)
                    act.wait_ge(S["q_rest"], b * PER["q_rest"] + a + 1)
                    A(q_parts[:, 1, :], rstd[:, :], ACT.Copy).then_inc(S["q_mid"], 1)
                    units, unit0 = score_units(a == 1), sum(N_SCORES[:a])
                    for what, pair, *rest in ORDER[a]:
                        if what == "rows":
                            act.wait_ge(S["max_turned"], b * PER["max_turned"] + PAIRS * a + pair + 1)
                            if pair > 0:
                                act.wait_ge(S["max_rows_in"], b * PER["max_rows_in"] + 48 * (PAIRS * a + pair))
                            A(banks3(max_rows[0:6, :]), PS[0:6, 5:8, 0:C3], ACT.Copy).then_inc(S["max_rows"], 1)
                        elif what == "exp":
                            qc, kb = units[rest[0]]
                            n = unit0 + pair * len(units) + rest[0]
                            s = max(0, P * kb - C3 * qc) if a == 1 else 0
                            act.wait_ge(S["scores"], b * PER["scores"] + n + 1)
                            if n >= unit0 + 3:
                                act.wait_ge(S["weights_used"], b * PER["weights_used"] + n - 2)
                            A(wts[:, n % 3, :, s:C3], PS[:, 2 * (n % 2):2 * (n % 2) + 2, s:C3], ACT.Exp).then_inc(S["weights"], 1)
                layer_norm(5)
                for m in range(4):
                    act.wait_ge(S["mlp_sum"], b * PER["mlp_sum"] + m + 1)
                    A(banks3(hidden[:, m, :]), slot(m % 2), ACT.Gelu, bias=w("m_b1")[:, m:m + 1]).then_inc(S["mlp_hidden"], 1)

        @block.vector
        def _(dve):
            tt, ts, stt = nc.vector.tensor_tensor, nc.vector.tensor_scalar, nc.vector.scalar_tensor_tensor
            dve.wait_ge(loaded, 48)
            nc.vector.tensor_copy(CB[:, :], consts_f32)
            for l in range(L):
                for j in range(TAPS):
                    x = tt(conv_wi[:, l, j, :], wi[:, l, 0:256], conv_w[:, l, j, :], ALU.mult)
            nc.vector.memset(h_pad[:, 0:3], 0.0).then_inc(convs_ready, 1)
            dve.wait_ge(decays_ready, 1)
            ts(a_neg[:, :], a_neg[:, :], -1.0, None, ALU.mult).then_inc(decays_ready, 1)
            with dve.Fori(0, B) as b:
                steps = [0]

                def step(instruction):
                    steps[0] += 1
                    instruction.then_inc(S["dve_step"], 1)
                    dve.wait_ge(S["dve_step"], b * PER["dve_step"] + steps[0])

                def layer_norm(i, src, dst, affine=None):
                    dve.wait_ge(S["ln_mean"], b * PER["ln_mean"] + i + 1)
                    tt(banks3(cen[:, :]), banks3(src), slot(0), ALU.subtract).then_inc(S["ln_centered"], 1)
                    dve.wait_ge(S["ln_std"], b * PER["ln_std"] + i + 1)
                    r, v, t = stats[:, 0:NB], stats[:, NB:2 * NB], stats[:, 2 * NB:3 * NB]
                    ts(v, PS[:, 6, 0:NB], EPS, None, ALU.add)
                    step(nc.vector.reciprocal(r, deviation))
                    step(tt(t, r, r, ALU.mult))
                    step(tt(t, t, v, ALU.mult))
                    step(ts(t, t, -0.5, 1.5, ALU.mult, ALU.add))
                    tt(r, r, t, ALU.mult).then_inc(S["ln_rstd"], 1)
                    dve.wait_ge(S["ln_bcast"], b * PER["ln_bcast"] + i + 1)
                    if affine is None:
                        return tt(banks3(dst), banks3(cen[:, :]), slot(1), ALU.mult)
                    step(tt(banks3(dst), banks3(cen[:, :]), slot(1), ALU.mult))
                    return ts(dst, dst, affine[0], affine[1], ALU.mult, ALU.add)

                dve.wait_ge(S["emb_sum"], b * PER["emb_sum"] + 1)
                pe_cols = w("pe")
                tt(h0[:, 0:2 * C3].rearrange("p (c t) -> p c t", c=2), PS[:, 0:2, 0:C3],
                   pe_cols[:, 0:2 * C3].rearrange("p (c t) -> p c t", c=2), ALU.add)
                tt(h0[:, 2 * C3:IMG], PS[:, 2, 0:IMG - 2 * C3], pe_cols[:, 2 * C3:IMG], ALU.add).then_inc(S["ln_src"], 1)
                dve.wait_ge(S["ln_src"], b * PER["ln_src"] + 1)
                layer_norm(0, h0[:, :], h_pad[:, 3:3 + T]).then_inc(S["ln_out"], 1)

                for l in range(L):
                    dve.wait_ge(S["bc_hi"], b * PER["bc_hi"] + l + 1)
                    stt(banks3(bc_rest[0:96, :]), banks3(bc_hi[0:96, :]), masks[0:96, 0:1], slot(0)[0:96],
                           ALU.mult, ALU.add).then_inc(S["bc_rest"], 1)
                    dve.wait_ge(S["bc_mid"], b * PER["bc_mid"] + l + 1)
                    stt(bc_parts[0:96, :], bc_mid[0:96, :], masks[0:96, 1:2], bc_rest[0:96, :],
                           ALU.mult, ALU.add).then_inc(S["bc_parts"], 1)
                    for u in range(U):
                        dve.wait_ge(S["dt_abs"], b * PER["dt_abs"] + 2 * l + u + 1)
                        ts(banks3(delta[:, u, :]), slot(1 - u), w("bdt")[:, 2 * l + u:2 * l + u + 1], 0.0,
                              ALU.add, ALU.max).then_inc(S["dt_read"], 1)
                    for u in range(U):
                        dve.wait_ge(S["dt_exp"], b * PER["dt_exp"] + 2 * l + u + 1)
                        e = dx[:, u, :]
                        ts(e_small, e, SMALL_E, None, ALU.is_lt)
                        ts(rstd[:, :], e, -0.5, 1.0, ALU.mult, ALU.add)
                        step(ts(sq[:, :], e, 1.0, 1.0, ALU.add, ALU.subtract))
                        tt(rstd[:, :], rstd[:, :], e, ALU.mult)
                        step(tt(sq[:, :], sq[:, :], e, ALU.subtract))
                        dve.wait_ge(S["dt_log"], b * PER["dt_log"] + 2 * l + u + 1)
                        step(tt(sq[:, :], gate[:, u, :], sq[:, :], ALU.subtract))
                        dve.sem_inc(S["log_waited"], 1)
                        step(nc.vector.copy_predicated(sq[:, :], e_small, rstd[:, :]))
                        tt(delta[:, u, :], delta[:, u, :], sq[:, :], ALU.add).then_inc(S["delta_ready"], 1)
                        dve.wait_ge(S["delta_ready"], b * PER["delta_ready"] + 2 * l + u + 1)
                        tt(dx[:, u, :], delta[:, u, :], xs[:, u, :], ALU.mult).then_inc(S["dx_ready"], 1)
                    dve.wait_ge(S["dx_ready"], b * PER["dx_ready"] + 2 * l + 2)

                    def drives(r):
                        t0 = ((r // NS) % 2) * TH
                        dve.wait_ge(S["b_bcast"], b * PER["b_bcast"] + r + 1)
                        if r >= 3:
                            dve.wait_ge(S["state_ready"], b * PER["state_ready"] + 2 * (r - 2))
                        bb = PS[:, 4:6, 0:TQ].unsqueeze(1).broadcast_to([P, U, 2, TQ])
                        tt(drive[r % 3].rearrange("p u (q t) -> p u q t", q=2),
                              dx[:, :, t0:t0 + TH].rearrange("p u (q t) -> p u q t", q=2), bb, ALU.mult).then_inc(S["input_ready"], 1)

                    def read_y(m):
                        t0 = (m % 2) * TH
                        dve.wait_ge(S["y_sum"], b * PER["y_sum"] + NS * (m + 1))
                        for u in range(U):
                            x = stt(gate[:, u, t0:t0 + TH].rearrange("p (q t) -> p q t", q=2),
                                    xs[:, u, t0:t0 + TH].rearrange("p (q t) -> p q t", q=2),
                                    w("d_skip")[:, 2 * l + u:2 * l + u + 1], PS[:, 2 * u:2 * u + 2, 0:TQ],
                                    ALU.mult, ALU.add)
                        x.then_inc(S["y_read"], 1)
                        dve.wait_ge(S["y_read"], b * PER["y_read"] + m + 1)
                        tt(gate[:, :, t0:t0 + TH], gate[:, :, t0:t0 + TH], zs[:, :, t0:t0 + TH], ALU.mult).then_inc(S["gated"], 1)

                    drives(32 * l)
                    for r in range(32 * l, 32 * l + 32):
                        k, n = (r // NS) % 2, r % NS
                        if r + 1 < 32 * l + 32:
                            drives(r + 1)
                        dve.wait_ge(S["decay_ready"], b * PER["decay_ready"] + 2 * r + 2)
                        dve.wait_ge(S["input_ready"], b * PER["input_ready"] + r + 1)
                        if r >= 3:
                            dve.wait_ge(S["out_ready"], b * PER["out_ready"] + r - 2)
                        for u in range(U):
                            init = 0.0 if k == 0 else last[:, u, n:n + 1]
                            nc.vector.tensor_tensor_scan(state[:, r % 3, u, :], decay[:, r % 2, u, :],
                                                            drive[r % 3][:, u, :], init, ALU.mult, ALU.add).then_inc(S["state_ready"], 1)
                        if k == 0:
                            dve.wait_ge(S["state_ready"], b * PER["state_ready"] + 2 * r + 2)
                            nc.vector.tensor_copy(last[:, :, n:n + 1], state[:, r % 3, :, TH - 1:TH]).then_inc(S["last_saved"], 1)
                            if n == NS - 1:
                                dve.wait_ge(S["last_saved"], b * PER["last_saved"] + NS * (l + 1))
                        if k == 1 and n == LAG - 1:
                            read_y(2 * l)
                    read_y(2 * l + 1)
                    dve.wait_ge(S["wo_sum"], b * PER["wo_sum"] + l + 1)
                    tt(banks3(res[:, :]), slot(0), banks3(h_pad[:, 3:3 + T]), ALU.add).then_inc(S["ln_src"], 1)
                    dve.wait_ge(S["ln_src"], b * PER["ln_src"] + l + 2)
                    g, bb = w("ln_g")[:, l:l + 1], w("ln_b")[:, l:l + 1]
                    layer_norm(l + 1, res[:, :], h_pad[:, 3:3 + T], (g, bb)).then_inc(S["ln_out"], 1)
                dve.wait_ge(S["ln_out"], b * PER["ln_out"] + 3)
                tt(h0[:, :], h0[:, :], h_pad[:, 3:3 + T], ALU.add).then_inc(S["ln_src"], 1)
                dve.wait_ge(S["ln_src"], b * PER["ln_src"] + 4)
                layer_norm(3, h0[:, :], res[:, :]).then_inc(S["ln_out"], 1)
                dve.wait_ge(S["ln_out"], b * PER["ln_out"] + 4)
                step(nc.vector.tensor_reduce(small[:, 2:3], res[:, :], AX.X, ALU.add))
                ts(small[:, 0:1], small[:, 2:3], 1.0 / T, None, ALU.mult).then_inc(S["pooled"], 1)
                dve.wait_ge(S["r_hidden"], b * PER["r_hidden"] + 1)
                nc.vector.tensor_copy(hidden_bc, small[:, 1:2].broadcast_to([P, P])).then_inc(S["r_bcast"], 1)
                dve.wait_ge(S["r_sum"], b * PER["r_sum"] + 1)
                lg = small[:, 8:16].rearrange("p (s e) -> p s e", s=2)
                hot = small[:, 16:24].rearrange("p (s e) -> p s e", s=2)
                top, free = small[:, 24:26], small[:, 26:28]
                step(tt(small[:, 8:16], PS[:, 7, 0:2 * EXP], w("r_b2"), ALU.add))
                step(nc.vector.tensor_reduce(top, lg, AX.X, ALU.max))
                step(tt(hot, lg, top.unsqueeze(2).broadcast_to([P, 2, EXP]), ALU.is_ge))
                step(ts(free, hot[:, :, 0], -1.0, 1.0, ALU.mult, ALU.add))
                for e in range(1, EXP):
                    step(tt(hot[:, :, e], hot[:, :, e], free, ALU.mult))
                    if e < EXP - 1:
                        step(tt(free, free, hot[:, :, e], ALU.subtract))
                for s in range(2):
                    cs = slice(s * AW, (s + 1) * AW)
                    step(ts(chosen[:, cs], expert[:, 0, cs], hot[:, s, 0:1], None, ALU.mult))
                    for e in range(1, EXP):
                        x = stt(chosen[:, cs], expert[:, e, cs], hot[:, s, e:e + 1], chosen[:, cs], ALU.mult, ALU.add)
                        if e < EXP - 1:
                            step(x)
                x.then_inc(S["chosen"], 1)
                layer_norm(4, res[:, :], s_out).then_inc(S["ln_out"], 1)
                dve.wait_ge(S["ln_out"], b * PER["ln_out"] + 5)
                ts(xhat, s_out, norms[:, 0:1], norms[:, 1:2], ALU.mult, ALU.add).then_inc(S["att_in"], 1)
                ts(t_in, s_out, norms[:, 2:3], norms[:, 3:4], ALU.mult, ALU.add).then_inc(S["att_in"], 1)

                for a in range(ATT):
                    dve.wait_ge(S["q_sum"], b * PER["q_sum"] + a + 1)
                    ts(banks3(cen[:, :]), slot(0), aw(a, "qb"), HD ** -0.5, ALU.add, ALU.mult).then_inc(S["q_read"], 1)
                    dve.wait_ge(S["k_hi"], b * PER["k_hi"] + a + 1)
                    tt(sq[:, :], qf, k_parts[:, 0, :], ALU.subtract).then_inc(S["k_rest"], 1)
                    dve.wait_ge(S["k_mid"], b * PER["k_mid"] + a + 1)
                    tt(k_parts[:, 2, :], sq[:, :], k_parts[:, 1, :], ALU.subtract).then_inc(S["k_parts"], 1)
                    dve.wait_ge(S["q_hi"], b * PER["q_hi"] + a + 1)
                    tt(rstd[:, :], cen[:, :], q_parts[:, 0, :], ALU.subtract).then_inc(S["q_rest"], 1)
                    dve.wait_ge(S["q_mid"], b * PER["q_mid"] + a + 1)
                    tt(q_parts[:, 2, :], rstd[:, :], q_parts[:, 1, :], ALU.subtract).then_inc(S["q_parts"], 1)
                    dve.wait_ge(S["v_sum"], b * PER["v_sum"] + a + 1)
                    vb = aw(a, "vb").rearrange("p (h c) -> p h c", h=HEADS)
                    for c in range(3):
                        for k in range(3):
                            x = tt(v_aug[:, 3 * c + k, :, 0:HD],
                                   PS[:, c, k * P:(k + 1) * P].rearrange("p (h c) -> p h c", h=HEADS), vb, ALU.add)
                    x.then_inc(S["v_read"], 1)
                    if a == 0:
                        nc.vector.memset(v_aug[:, :, :, HD:32], 1.0)
                        nc.vector.memset(k_stack[KQ:KQ + 3, :, :], 1.0).then_inc(S["ones_ready"], 1)
                    units, tops = score_units(a == 1), max_units(a == 1)
                    top0, unit0 = sum(N_MAX[:a]), sum(N_SCORES[:a])
                    for what, pair, *rest in ORDER[a]:
                        if what == "max":
                            j, qb, c = tops[rest[0]]
                            m = top0 + pair * len(tops) + rest[0]
                            cols = min(C3, P * (qb + 1) - C3 * c) if a == 1 else C3
                            dve.wait_ge(S["max_scores"], b * PER["max_scores"] + m + 1)
                            nc.vector.tensor_reduce(max3[:, pair, qb, j, c:c + 1], PS[:, 5 + m % 3, 0:cols],
                                                       AX.X, ALU.max).then_inc(S["max_read"], 1)
                        elif what == "split":
                            dve.wait_ge(S["max_read"], b * PER["max_read"] + top0 + (pair + 1) * len(tops))
                            for c in range(3):
                                ks = slice(3 * c, 3 * c + 3)
                                x = nc.vector.tensor_reduce(max_tmp[:, pair, ks, :],
                                                            max3[:, pair, ks, :, 0:(c + 1 if a == 1 else 3)],
                                                            AX.X, ALU.max)
                            step(x)
                            low, parts = max_tmp[:, pair], max_parts[:, pair]
                            step(ts(neg_max[:, pair], low, -1.0, None, ALU.mult))
                            step(nc.vector.tensor_copy(parts[:, :, 0, :], neg_max[:, pair]))
                            step(tt(low, neg_max[:, pair], parts[:, :, 0, :], ALU.subtract))
                            step(nc.vector.tensor_copy(parts[:, :, 1, :], low))
                            tt(parts[:, :, 2, :], low, parts[:, :, 1, :], ALU.subtract).then_inc(S["max_split"], 1)
                        elif what == "read":
                            qc = rest[0]
                            o = 64 * (pair % 2)
                            done = sum(1 for u in units if u[0] <= qc)
                            dve.wait_ge(S["weights_used"], b * PER["weights_used"] + unit0 + pair * len(units) + done)
                            nc.vector.tensor_copy(heads_o[o:o + 64, pair // 2, qc * C3:(qc + 1) * C3],
                                                     PS[o:o + 64, 4, 0:C3]).then_inc(S["heads_read"], 1)
                    dve.wait_ge(S["denom"], b * PER["denom"] + a + 1)
                    step(nc.vector.reciprocal(inverse, PS[:, 6, 0:8 * NB]))
                    nc.vector.tensor_copy(inverse_rows.rearrange("p (h c) -> p h c", c=32),
                                             inverse.unsqueeze(2).broadcast_to([P, 8 * NB, 32])).then_inc(S["denom_inv"], 1)
                    for g in range(2):
                        dve.wait_ge(S["denom_bcast"], b * PER["denom_bcast"] + 2 * a + g + 1)
                        tt(banks3(heads_o[:, g, :]), banks3(heads_o[:, g, :]), slot(g), ALU.mult).then_inc(S["heads_out"], 1)
                    dve.wait_ge(S["proj_sum"], b * PER["proj_sum"] + a + 1)
                    if a == 0:
                        ts(banks3(s_out), slot(0), aw(a, "ob"), None, ALU.add).then_inc(S["att_out"], 1)
                    elif a == 1:
                        stt(banks3(t_out), slot(0), aw(a, "ob"), banks3(t_in), ALU.add, ALU.add).then_inc(S["att_out"], 1)
                    else:
                        stt(banks3(res[:, :]), slot(0), aw(a, "ob"), banks3(res[:, :]), ALU.add, ALU.add).then_inc(S["ln_src"], 1)
                dve.wait_ge(S["ln_src"], b * PER["ln_src"] + 5)
                layer_norm(5, res[:, :], xhat, (norms[:, 4:5], norms[:, 5:6])).then_inc(S["ln_out"], 1)
                step(tt(h0[:, :], h0[:, :], res[:, :], ALU.add))
                dve.wait_ge(S["mlp_out_sum"], b * PER["mlp_out_sum"] + 1)
                stt(banks3(result[:, :]), slot(0), w("m_b2"), banks3(h0[:, :]), ALU.add, ALU.add).then_inc(S["result"], 1)

        @block.gpsimd
        def _(pool):
            with pool.Fori(0, B) as b:
                for r in range(64):
                    pool.wait_ge(S["state_ready"], b * PER["state_ready"] + 2 * r + 2)
                    pool.wait_ge(S["c_copied"], b * PER["c_copied"] + r + 1)
                    if r >= OUTS:
                        pool.wait_ge(S["y_sum"], b * PER["y_sum"] + r - OUTS + 1)
                    cc = c_sb[:, r % 3, :].unsqueeze(1).broadcast_to([P, U, TH])
                    nc.gpsimd.tensor_tensor(outs[:, r % OUTS, :, :], state[:, r % 3, :, :], cc, ALU.mult).then_inc(S["out_ready"], 1)


def pack(i):
    f = {k: np.asarray(v) for k, v in i.items()}
    parts = {}
    bc = lambda v: np.broadcast_to(v, (P, v.size))
    tall = lambda v: np.pad(v, ((0, P - v.shape[0]), (0, 0)))
    cols = lambda v: np.ascontiguousarray(v.reshape(-1, P).T)
    parts["tok_w"] = tall(f["L0_tok_W"])
    pos = np.arange(2 * IMG, dtype=np.float32)[:, None]
    div = np.exp(np.arange(0, D, 2, dtype=np.float32) * (-math.log(10000.0) / D))
    pe = np.zeros((2 * IMG, D), np.float32)
    pe[:, 0::2], pe[:, 1::2] = np.sin(pos * div), np.cos(pos * div)
    parts["pe"] = pe[:IMG].T
    parts["wi"] = f["L0_attn_in_proj_w"].transpose(1, 0, 2).reshape(P, -1)
    parts["conv_w"] = bc(f["L0_attn_conv_w"][:, :, 0, :].transpose(0, 2, 1).reshape(-1))
    parts["conv_b"] = cols(f["L0_attn_conv_b"])
    wx = f["L0_attn_x_proj_w"]
    wx = np.concatenate([wx[:, :, RANK:]] * 3 + [wx[:, :, :RANK]], axis=2)
    parts["wx"] = wx.reshape(L, U, P, SR).transpose(2, 0, 1, 3).reshape(P, -1)
    wdt = f["L0_attn_dt_proj_w"].transpose(1, 0, 2).reshape(RANK, -1)
    parts["wdt"] = np.pad(wdt, ((96, P - 96 - RANK), (0, 0)))
    parts["bdt"] = cols(f["L0_attn_dt_proj_b"])
    parts["a_log"] = f["L0_attn_A_log"].reshape(L, U, P, NS).transpose(2, 0, 1, 3).reshape(P, -1)
    parts["d_skip"] = cols(f["L0_attn_D_skip"])
    parts["wo"] = f["L0_attn_out_proj_w"].reshape(L, U, P, D).transpose(2, 0, 1, 3).reshape(P, -1)
    parts["ln_g"], parts["ln_b"] = f["L0_attn_ln_g"].T, f["L0_attn_ln_b"].T
    parts["r_w1"] = f["L0_ffn_router_w1"].T
    parts["r_b1"] = f["L0_ffn_router_b1"][:, None]
    parts["r_w2"] = f["L0_ffn_router_w2"].T
    parts["r_b2"] = bc(f["L0_ffn_router_b2"])
    parts["norms"] = np.stack([f["L0_ffn_" + n] for n in ("norm_s_w", "norm_s_b", "norm_t_w", "norm_t_b",
                                                          "norm_mlp_w", "norm_mlp_b")], axis=1)

    def attention(wq, wk, wv, bq, bk, bv, w_out, b_out):
        o = np.zeros((2, 4, 32, P), np.float32)
        o[:, :, :HD, :] = w_out.T.reshape(2, 4, HD, P)
        o = o.reshape(2 * P, P)
        return np.concatenate([wq.T, wk.T, wv.T, bc(bv), o[:P], o[P:], bq[:, None], bk[:, None], b_out[:, None]], 1)

    sides = []
    for e in range(EXP):
        win, bin_ = f["L0_ffn_sp_in_w"][e], f["L0_ffn_sp_in_b"][e]
        sides.append(attention(win[:D], win[D:2 * D], win[2 * D:], bin_[:D], bin_[D:2 * D], bin_[2 * D:],
                               f["L0_ffn_sp_out_w"][e], f["L0_ffn_sp_out_b"][e]))
        sides.append(attention(*(f[f"L0_ffn_t{n}_w"][e] for n in "qkv"), *(f[f"L0_ffn_t{n}_b"][e] for n in "qkv"),
                               f["L0_ffn_tp_w"][e], f["L0_ffn_tp_b"][e]))
    parts["expert"] = np.concatenate(sides, axis=1)
    win, bin_ = f["L0_ffn_cross_in_w"], f["L0_ffn_cross_in_b"]
    parts["cross"] = attention(win[:D], win[D:2 * D], win[2 * D:], bin_[:D], bin_[D:2 * D], bin_[2 * D:],
                               f["L0_ffn_cross_out_w"], f["L0_ffn_cross_out_b"])
    parts["m_w1"] = f["L0_ffn_mlp_w1"].T
    parts["m_b1"] = cols(f["L0_ffn_mlp_b1"])
    parts["m_w2"] = f["L0_ffn_mlp_w2"].T.reshape(4, P, D).transpose(1, 0, 2).reshape(P, -1)
    parts["m_b2"] = f["L0_ffn_mlp_b2"][:, None]
    parts["mean_mat"] = np.full((P, P), 1.0 / D, np.float32)
    parts["identf"] = np.eye(P, dtype=np.float32)
    sum_row = np.zeros((P, 4), np.float32)
    for h in range(4):
        sum_row[32 * h + HD, h] = 1.0
    parts["sum_row"] = sum_row
    masks = np.zeros((P, 2), np.float32)
    masks[32:, 0] = -1.0
    masks[64:, 1] = -1.0
    parts["masks"] = masks
    parts["eps"] = np.full((P, 1), EPS, np.float32)
    out = np.concatenate([parts[n] for n, _ in _F32], axis=1)
    assert out.shape == (P, F32_COLS) and out.dtype == np.float32
    return np.ascontiguousarray(out)


def constants():
    pick = np.zeros((P, 2 * NS, P), np.float32)
    for n in range(2 * NS):
        pick[[n, 32 + n, 64 + n], n, :] = 1.0
    late = np.triu(np.full((P, P), -1e38, np.float32), 1)
    return np.concatenate([np.eye(P, dtype=np.float32), late, late.T, pick.reshape(P, -1)], axis=1)


def kernel(**inputs):
    import concourse.bacc as _bacc
    from concourse.bass_utils import run_bass_kernel_spmd as _run

    B = inputs["x"].shape[0]
    arrays = {
        "xT": np.ascontiguousarray(np.asarray(inputs["x"]).reshape(B, IMG, FEAT).transpose(0, 2, 1)),
        "txtT": np.ascontiguousarray(np.asarray(inputs["txt"]).transpose(0, 2, 1)),
        "params": pack({k: v for k, v in inputs.items() if k not in ("x", "txt")}),
        "consts": constants(),
    }
    nc = _bacc.Bacc("TRN2", target_bir_lowering=False, num_devices=1)
    args = [nc.dram_tensor(n, a.shape, mybir.dt.from_np(a.dtype), kind="ExternalInput").ap()
            for n, a in arrays.items()]
    out = nc.dram_tensor("outT", (B, D, T), mybir.dt.float32, kind="ExternalOutput").ap()
    fusion_kernel(nc, *args, out)
    r = _run(nc, [arrays], core_ids=[0])
    return np.ascontiguousarray(r.results[0]["outT"].transpose(0, 2, 1))
```

```python
import math

import numpy as np

import concourse.bass as bass
from concourse import mybir
from contextlib import ExitStack

P = 128
TXT, IMG = 128, 1024
T = TXT + IMG
D = 128
FEAT = 29
L = 2
TAPS, NS, RANK = 4, 16, 8
U = 2
HEADS, HD = 8, 16
EXP = 4
NB = T // P
C3 = 384
TH = T // 2
TQ = TH // 2
EPS = 1e-5
SMALL_E = 2.0 ** -10
LAG = 3
OUTS = 4
Q_PART = (0, 0, 1, 1, 0, 2)
K_PART = (0, 1, 0, 1, 2, 0)
KQ = 6 * HD
SR = 3 * 32 + RANK
ATT = 3
AW = 6 * P + 3

_F32 = [
    ("tok_w", D), ("pe", IMG), ("wi", L * 512), ("conv_b", L * U),
    ("wx", L * U * SR), ("wdt", L * 256), ("bdt", L * U), ("a_log", L * U * NS), ("d_skip", L * U),
    ("wo", L * U * D), ("ln_g", L), ("ln_b", L), ("r_w1", D), ("r_b1", 1), ("r_w2", 2 * EXP),
    ("r_b2", 2 * EXP), ("norms", 6), ("expert", EXP * 2 * AW), ("cross", AW), ("m_w1", 4 * D),
    ("m_b1", 4), ("m_w2", 4 * D), ("m_b2", 1), ("mean_mat", P), ("identf", P), ("sum_row", 4),
    ("masks", 2), ("eps", 1), ("conv_w", L * TAPS * 256),
]
F32_AT = {}
_n = 0
for _name, _w in _F32:
    F32_AT[_name] = (_n, _n + _w)
    _n += _w
F32_COLS = _n
KEPT_COLS = F32_AT["conv_w"][0]
BF_COLS = 3 * P + 2 * NS * P

PER = dict(
    tokens_in=32, emb_sum=1, ln_src=5, ln_mean=6, ln_centered=6, ln_squared=6, ln_var=6, ln_std=6, ln_rstd=6, ln_bcast=6, ln_out=6,
    xc_sum=4, z_sum=4, xs_ready=4, zs_ready=4, dbc_sum=2, bc_hi=2, bc_rest=2, bc_mid=2, bc_parts=2,
    dt_rows=2, dt_sum=4, dt_abs=4, dt_read=4, dt_exp=4, dt_log=4, delta_ready=4, dx_ready=4,
    b_bcast=64, c_bcast=64, c_copied=64, decay_ready=128, input_ready=64, state_ready=128,
    out_ready=64, y_sum=64, y_read=4, gated=4, wo_sum=2,
    pooled=1, r_hidden_sum=1, r_hidden=1, r_bcast=1, r_sum=1, chosen=1,
    att_in=2, q_sum=3, k_sum=3, v_sum=3, q_read=3, k_read=3, v_read=3,
    q_hi=3, q_rest=3, q_mid=3, q_parts=3, k_hi=3, k_rest=3, k_mid=3, k_parts=3,
    k_hi_out=48, k_mid_out=48, k_low_out=48, q_hi_out=48, q_mid_out=48, q_low_out=48, ones_in=16, k_stacks_in=3 * 6 * 16, q_stacks_in=3 * 6 * 16, max_rows_in=0,
    max_scores=0, max_read=0, max_split=0, max_turned=0, max_rows=0,
    scores=0, weights=0, weights_used=0, heads_read=0, denom=3, denom_inv=3, denom_bcast=6, heads_out=6, proj_sum=3, att_out=2,
    mlp_sum=4, mlp_hidden=4, mlp_out_sum=1, result=1, stored=16,
    dve_step=0, log_waited=4, last_saved=32, ones_ready=1,
)


def score_units(causal):
    return [(qc, kb) for qc in range(3) for kb in range(min(NB, 3 * qc + 3) if causal else NB)]


def halves(causal, qc):
    return 1 if causal and qc == 0 else 2


def max_units(causal):
    return [(j, qb, c) for j in range(2) for qb in range(NB) for c in range(qb // 3 + 1 if causal else 3)]


def helped(causal, pair, qb):
    return pair == 0 and (not causal or qb >= 6)


def attention_order(causal):
    units, tops = score_units(causal), max_units(causal)
    order = [("max", 0, i) for i in range(len(tops))] + [("split", 0), ("turn", 0), ("rows", 0)]
    ahead = []
    for pair in range(1, PAIRS):
        ahead += [("max", pair, i) for i in range(len(tops))] + [("split", pair), ("turn", pair), ("rows", pair)]
    taken = 0.0
    for pair in range(PAIRS):
        for i in range(len(units) + 1):
            if i < len(units):
                order.append(("exp", pair, i))
                taken += len(tops) / (len(units) - (6 if ahead and ahead[0][1] == 1 else 4))
                while ahead and ahead[0][0] == "max" and taken >= 1:
                    order.append(ahead.pop(0))
                    taken -= 1
                if ahead and ahead[0][0] != "max":
                    order.append(ahead.pop(0))
                    taken = 0.0
            if i > 0:
                qc, kb = units[i - 1]
                ends = i == len(units) or units[i][0] != qc
                if ends and kb % 2 == 0:
                    order.append(("weigh", pair, i - 1))
                elif kb % 2 == 1:
                    order += [("weigh", pair, i - 2), ("weigh", pair, i - 1)]
                if ends:
                    order.append(("read", pair, qc))
    return order


PAIRS = HEADS // 2
ORDER = [attention_order(a == 1) for a in range(ATT)]
N_SCORES = [PAIRS * len(score_units(a == 1)) for a in range(ATT)]
N_MAX = [PAIRS * len(max_units(a == 1)) for a in range(ATT)]
COPIED = [helped(a == 1, pair, qb) and c == 0
          for a in range(ATT) for pair in range(PAIRS) for j, qb, c in max_units(a == 1)]
GROUP_ENDS = [helped(a == 1, pair, qb) and c == 2 and not (qb % 3 < 2 and helped(a == 1, pair, qb + 1))
              for a in range(ATT) for pair in range(PAIRS) for j, qb, c in max_units(a == 1)]
COPIES = [sum(COPIED[:m]) for m in range(len(COPIED) + 1)]
READS = [m - COPIES[m] for m in range(len(COPIED) + 1)]
GROUPS = [sum(GROUP_ENDS[:m]) for m in range(len(COPIED) + 1)]
MAX_BANK = [(5, 6, 7, 0, 1, 2, 3)[i % 7] if pair == 0 else 5 + i % 3
            for a in range(ATT) for pair in range(PAIRS) for i in range(len(max_units(a == 1)))]


def bank_before(m, first):
    return next((n for n in range(m - 1, first - 1, -1) if MAX_BANK[n] == MAX_BANK[m]), None)


SCORE_BANKS = [(2 * (i % 2) if pair < PAIRS - 1 or i < 2 else (0, 2, 5)[i % 3])
               for a in range(ATT) for pair in range(PAIRS) for i in range(len(score_units(a == 1)))]


def scores_before(n, first):
    return next((m for m in range(n - 1, first - 1, -1) if SCORE_BANKS[m] == SCORE_BANKS[n]), None)


PER["scores"] = PER["weights"] = PER["weights_used"] = sum(N_SCORES)
PER["max_scores"], PER["max_copied"], PER["max_read"] = sum(N_MAX), COPIES[-1], READS[-1]
PER["tops_kept"] = GROUPS[-1]
PER["heads_read"] = ATT * PAIRS * 3
READ_COPIES = [sum(halves(a == 1, qc) == 2 for a in range(ATT) for pair in range(PAIRS) for qc in range(3)
                   if (a, pair, qc) < (a1, p1, q1)) for a1 in range(ATT) for p1 in range(PAIRS) for q1 in range(3)]
PER["heads_copied"] = READ_COPIES[-1] + 1
PER["max_split"] = PER["max_turned"] = PER["max_rows"] = ATT * PAIRS
PER["max_rows_in"] = ATT * PAIRS * 3 * 16
PER["dve_step"] = 123


def fusion_kernel(nc, xT, txtT, params, consts, out):
    f32, bf16 = mybir.dt.float32, mybir.dt.bfloat16
    ALU = mybir.AluOpType
    ACT = mybir.ActivationFunctionType
    AX = mybir.AxisListType
    B = xT.shape[0]
    ctx = ExitStack()
    with ctx:
        def sb(name, shape, dt=f32):
            return ctx.enter_context(nc.sbuf_tensor(name, shape, dt))

        S = {name: ctx.enter_context(nc.semaphore(name)) for name in PER}
        loaded = ctx.enter_context(nc.semaphore("loaded"))
        convs_ready = ctx.enter_context(nc.semaphore("convs_ready"))
        decays_ready = ctx.enter_context(nc.semaphore("decays_ready"))

        W = sb("W", [P, KEPT_COLS])
        CB = sb("CB", [P, BF_COLS], bf16)
        conv_wi = sb("conv_wi", [P, L, TAPS, 256])
        a_neg = sb("a_neg", [P, L * U * NS])
        h_pad = sb("h_pad", [P, 3 + T])
        h0 = sb("h0", [P, T])
        res = sb("res", [P, T])
        cen = sb("cen", [P, T])
        sq = sb("sq", [P, T])
        rstd = sb("rstd", [P, T])
        result = sb("result_sb", [P, T])
        stats = sb("stats", [P, 4 * NB])
        deviation = stats[:, 3 * NB:4 * NB]
        ARENA = 28200
        arena = sb("arena", [P, ARENA])
        at = [0]

        def part(n):
            at[0] += n
            assert at[0] <= ARENA, at
            return arena[:, at[0] - n:at[0]]

        xs = part(U * T).rearrange("p (u t) -> p u t", u=U)
        zs = part(U * T).rearrange("p (u t) -> p u t", u=U)
        delta = part(U * T).rearrange("p (u t) -> p u t", u=U)
        dx = part(U * T).rearrange("p (u t) -> p u t", u=U)
        gate = part(U * T).rearrange("p (u t) -> p u t", u=U)
        bc_rest = part(T)
        bc_hi = cen[:, 0:T // 2].bitcast(bf16)
        bc_mid = cen[:, T // 2:T].bitcast(bf16)
        bc_parts = part(T // 2).bitcast(bf16)
        dt_rows = bc_rest
        e_small = result[:, 0:T // 4].bitcast(mybir.dt.uint8)
        decay = part(2 * U * TH).rearrange("p (r u t) -> p r u t", r=2, u=U)
        drive = [buf[:, :].rearrange("p (u t) -> p u t", u=U) for buf in (sq, rstd, cen)]
        state = part(3 * U * TH).rearrange("p (r u t) -> p r u t", r=3, u=U)
        outs = part(OUTS * U * TH).rearrange("p (r u t) -> p r u t", r=OUTS, u=U)
        c_sb = part(3 * TH).rearrange("p (r t) -> p r t", r=3)
        last = part(U * NS).rearrange("p (u n) -> p u n", u=U)
        at[0] = 0
        q_stack = part(HEADS * T // 2).bitcast(bf16).rearrange("p (h t) -> p h t", h=HEADS)
        k_stack = part(HEADS * T // 2).bitcast(bf16).rearrange("p (h t) -> p h t", h=HEADS)
        v_aug = part(NB * HEADS * 32).rearrange("p (k h c) -> p k h c", k=NB, h=HEADS)
        q_parts = part(3 * T // 2).bitcast(bf16).rearrange("p (s t) -> p s t", s=3)
        k_parts = part(3 * T // 2).bitcast(bf16).rearrange("p (s t) -> p s t", s=3)
        wts = [part(2 * C3).rearrange("p (i t) -> p i t", i=2) for _ in range(3)]
        wts.append(rstd[:, 0:2 * C3].rearrange("p (i t) -> p i t", i=2))
        odd_sums = rstd[:, 2 * C3:3 * C3]
        inverse_rows = arena[:, at[0] - 3 * 2 * C3:at[0]]
        heads_o = part(2 * T).rearrange("p (g t) -> p g t", g=2)
        xhat = part(T)
        s_out = part(T)
        t_in = part(T)
        t_out = part(T)
        qf = part(T)
        chosen = part(2 * AW)
        hidden_bc = part(P)
        small = part(64)
        inverse = part(8 * NB)
        max3 = part(NB * HEADS * 3).rearrange("p (r k h c) -> p r k h c", r=4, k=NB, h=2)
        neg_max = part(NB * HEADS).rearrange("p (r k h) -> p r k h", r=4, k=NB)
        max_tmp = part(NB * HEADS).rearrange("p (r k h) -> p r k h", r=4, k=NB)
        max_parts = part(3 * NB * HEADS // 2).bitcast(bf16).rearrange("p (r k s h) -> p r k s h", r=4, k=NB, s=3)
        max_rows = part(T // 2).bitcast(bf16)
        hidden = arena[:, 0:4 * T].rearrange("p (m t) -> p m t", m=4)

        tokens = arena[0:FEAT, 4 * T:4 * T + IMG]
        texts = arena[:, 4 * T + IMG:5 * T]

        PS = ctx.enter_context(nc.psum_tensor("PS", [P, 8, 512], f32))

        def slot(n, rows=P):
            return PS[0:rows, 3 * n:3 * n + 3, 0:C3]

        def banks3(ap):
            return ap.rearrange("p (c t) -> p c t", c=3)

        ones_dram = nc.dram_tensor("ones_dram", (3, HEADS, T), bf16, kind="Internal")
        parts_dram = nc.dram_tensor("parts_dram", (2, P, 3, T), bf16, kind="Internal")

        def w(name):
            a, z = F32_AT[name]
            return W[:, a:z]

        tok_w = w("tok_w")[0:FEAT, :]
        wi = w("wi").rearrange("p (l n) -> p l n", l=L)
        consts_f32 = arena[:, L * TAPS * 256:L * TAPS * 256 + BF_COLS]
        conv_w = arena[:, 0:L * TAPS * 256].rearrange("p (l j n) -> p l j n", l=L, j=TAPS)
        wx = w("wx").rearrange("p (l u n) -> p l u n", l=L, u=U)
        wdt = w("wdt").rearrange("p (l n) -> p l n", l=L)
        wo = w("wo").rearrange("p (l u n) -> p l u n", l=L, u=U)
        norms = w("norms")
        expert = w("expert").rearrange("p (e a) -> p e a", e=EXP)
        cross = w("cross")
        mean_mat, identf, sum_row, masks = w("mean_mat"), w("identf"), w("sum_row"), w("masks")
        ident, mask_q, mask_k = CB[:, 0:P], CB[:, P:2 * P], CB[:, 2 * P:3 * P]
        pick = CB[0:96, 3 * P:].rearrange("p (n m) -> p n m", n=2 * NS)

        def aw(a, what):
            base = cross if a == 2 else chosen[:, a * AW:(a + 1) * AW]
            cols = dict(q=(0, P), k=(P, 2 * P), v=(2 * P, 3 * P), vb=(3 * P, 4 * P), o0=(4 * P, 5 * P),
                        o1=(5 * P, 6 * P), qb=(6 * P, 6 * P + 1), kb=(6 * P + 1, 6 * P + 2),
                        ob=(6 * P + 2, 6 * P + 3))[what]
            return base[:, cols[0]:cols[1]]

        def att_q(a):
            return [xhat, t_in, s_out][a]

        def att_kv(a):
            return [xhat, t_in, t_out][a]

        top_buffers = [cen[:, :], sq[:, :]]

        def top_slot(m, qb):
            return top_buffers[GROUPS[m] % 2][:, (qb % 3) * C3:(qb % 3 + 1) * C3]

        block = ctx.enter_context(nc.Block())

        @block.sync
        def _(sp):
            sp.dma_start(W[:, :], params[:, 0:KEPT_COLS]).then_inc(loaded, 16)
            sp.dma_start(arena[:, 0:L * TAPS * 256], params[:, KEPT_COLS:F32_COLS]).then_inc(loaded, 16)
            sp.dma_start(consts_f32, consts).then_inc(loaded, 16)
            sp.wait_ge(convs_ready, 2)
            sp.dma_start(ones_dram[:, :, :], k_stack[KQ:KQ + 3, :, :]).then_inc(loaded, 16)
            sp.wait_ge(loaded, 64)

            def load(b):
                sp.dma_start(tokens, xT[bass.ds(b, 1), :, :].rearrange("o f t -> (o f) t")).then_inc(S["tokens_in"], 16)
                sp.dma_start(texts, txtT[bass.ds(b, 1), :, :].rearrange("o f t -> (o f) t")).then_inc(S["tokens_in"], 16)

            def element(b, more):
                for a in range(ATT):
                    def out_part(n, s, part):
                        return sp.dma_start(parts_dram[n, :, s, :], part[:, s, :])

                    def stack_part(n, s, dst):
                        src = parts_dram[n, :, s, :].rearrange("(h d) t -> d h t", h=HEADS)
                        for j in range(6):
                            if (Q_PART, K_PART)[n][j] == s:
                                sp.dma_start(dst[HD * j:HD * (j + 1), :, :], src).then_inc(S[("q_stacks_in", "k_stacks_in")[n]], 16)

                    sp.wait_ge(S["k_hi"], b * PER["k_hi"] + a + 1)
                    out_part(1, 0, k_parts).then_inc(S["k_hi_out"], 16)
                    sp.wait_ge(S["k_mid"], b * PER["k_mid"] + a + 1)
                    out_part(1, 1, k_parts).then_inc(S["k_mid_out"], 16)
                    if a == 0:
                        sp.dma_start(k_stack[KQ:KQ + 3, :, :], ones_dram[:, :, :]).then_inc(S["ones_in"], 16)
                    sp.wait_ge(S["k_hi_out"], b * PER["k_hi_out"] + 16 * (a + 1))
                    stack_part(1, 0, k_stack)
                    sp.wait_ge(S["k_parts"], b * PER["k_parts"] + a + 1)
                    out_part(1, 2, k_parts).then_inc(S["k_low_out"], 16)
                    sp.wait_ge(S["q_hi"], b * PER["q_hi"] + a + 1)
                    out_part(0, 0, q_parts).then_inc(S["q_hi_out"], 16)
                    sp.wait_ge(S["k_mid_out"], b * PER["k_mid_out"] + 16 * (a + 1))
                    stack_part(1, 1, k_stack)
                    sp.wait_ge(S["k_low_out"], b * PER["k_low_out"] + 16 * (a + 1))
                    stack_part(1, 2, k_stack)
                    sp.wait_ge(S["q_mid"], b * PER["q_mid"] + a + 1)
                    out_part(0, 1, q_parts).then_inc(S["q_mid_out"], 16)
                    sp.wait_ge(S["q_hi_out"], b * PER["q_hi_out"] + 16 * (a + 1))
                    stack_part(0, 0, q_stack)
                    sp.wait_ge(S["q_parts"], b * PER["q_parts"] + a + 1)
                    out_part(0, 2, q_parts).then_inc(S["q_low_out"], 16)
                    sp.wait_ge(S["q_mid_out"], b * PER["q_mid_out"] + 16 * (a + 1))
                    stack_part(0, 1, q_stack)
                    sp.wait_ge(S["q_low_out"], b * PER["q_low_out"] + 16 * (a + 1))
                    stack_part(0, 2, q_stack)
                    for pair in range(PAIRS):
                        sp.wait_ge(S["max_rows"], b * PER["max_rows"] + PAIRS * a + pair + 1)
                        for s in range(3):
                            sp.dma_start(q_stack[KQ + s:KQ + s + 1, 2 * pair:2 * pair + 2, :],
                                            max_rows[2 * s:2 * s + 2, :]).then_inc(S["max_rows_in"], 16)
                if more:
                    sp.wait_ge(S["ln_src"], b * PER["ln_src"] + 5)
                    load(b + 1)
                sp.wait_ge(S["result"], b * PER["result"] + 1)
                sp.dma_start(out[bass.ds(b, 1), :, :].rearrange("o f t -> (o f) t"), result[:, :]).then_inc(S["stored"], 16)
            load(0)
            with sp.Fori(0, B - 1) as b:
                element(b, True)
            element(B - 1, False)
            sp.wait_ge(S["stored"], 16 * B)

        @block.tensor
        def _(pe):
            mm = nc.tensor.matmul
            pe.wait_ge(loaded, 48)
            pe.wait_ge(convs_ready, 1)

            def dense(n, pairs, rows=P):
                for c in range(3):
                    for i, (lhsT, rhs) in enumerate(pairs):
                        x = mm(PS[0:rows, 3 * n + c, 0:C3], lhsT, rhs[:, c * C3:(c + 1) * C3],
                               start=(i == 0), stop=(i == len(pairs) - 1))
                return x

            def keep_warm(n):
                for _ in range(n):
                    mm(PS[:, 4, :], ident, CB[:, 3 * P:3 * P + 512], start=True, stop=True)

            with pe.Fori(0, B) as b:
                def layer_norm(i, src, ready, k, meanwhile=None):
                    pe.wait_ge(S[ready], b * PER[ready] + k)
                    dense(0, [(mean_mat, src)]).then_inc(S["ln_mean"], 1)
                    if meanwhile:
                        meanwhile()
                    pe.wait_ge(S["ln_squared"], b * PER["ln_squared"] + i + 1)
                    for k in range(NB):
                        x = mm(PS[:, 6, k:k + 1], sq[:, k * P:(k + 1) * P], mean_mat[:, 0:1], start=True, stop=True)
                    x.then_inc(S["ln_var"], 1)
                    pe.wait_ge(S["ln_rstd"], b * PER["ln_rstd"] + i + 1)
                    for k in range(NB):
                        x = mm(PS[:, 3 + k // 3, (k % 3) * P:(k % 3 + 1) * P], stats[:, k:k + 1].broadcast_to([P, P]),
                               identf, start=True, stop=True)
                    x.then_inc(S["ln_bcast"], 1)

                pe.wait_ge(S["tokens_in"], b * PER["tokens_in"] + 32)
                pe.wait_ge(S["result"], b * PER["result"])
                for c, (s, e) in enumerate(((0, C3), (C3, 2 * C3), (2 * C3, IMG))):
                    x = mm(PS[:, c, 0:e - s], tok_w, tokens[:, s:e], start=True, stop=True)
                x.then_inc(S["emb_sum"], 1)
                layer_norm(0, h0, "ln_src", 1)

                for l in range(L):
                    pe.wait_ge(S["ln_out"], b * PER["ln_out"] + l + 1)
                    for u in range(U):
                        dense(u, [(conv_wi[:, l, j, u * P:(u + 1) * P], h_pad[:, j:j + T])
                                     for j in range(TAPS)]).then_inc(S["xc_sum"], 1)
                    pe.wait_ge(S["xs_ready"], b * PER["xs_ready"] + 2 * l + 2)
                    dense(0, [(wx[:, l, u, :], xs[:, u, :]) for u in range(U)], SR).then_inc(S["dbc_sum"], 1)
                    dense(1, [(wi[:, l, 256:256 + P], h_pad[:, 3:3 + T])]).then_inc(S["z_sum"], 1)
                    pe.wait_ge(S["dt_rows"], b * PER["dt_rows"] + l + 1)
                    pe.wait_ge(S["zs_ready"], b * PER["zs_ready"] + 2 * l + 1)
                    for u in range(U):
                        if u == 1:
                            pe.wait_ge(S["bc_rest"], b * PER["bc_rest"] + l + 1)
                            pe.wait_ge(S["bc_hi"], b * PER["bc_hi"] + l + 1)
                        dense(1 - u, [(wdt[96:96 + RANK, l, u * P:(u + 1) * P], dt_rows[96:96 + RANK, :])]).then_inc(S["dt_sum"], 1)
                    pe.wait_ge(S["dt_read"], b * PER["dt_read"] + 2 * l + 1)
                    dense(1, [(wi[:, l, 256 + P:512], h_pad[:, 3:3 + T])]).then_inc(S["z_sum"], 1)
                    pe.wait_ge(S["bc_parts"], b * PER["bc_parts"] + l + 1)
                    pe.wait_ge(S["dt_read"], b * PER["dt_read"] + 2 * l + 2)
                    pe.wait_ge(S["zs_ready"], b * PER["zs_ready"] + 2 * l + 2)

                    def accumulate(r):
                        k, n = (r // NS) % 2, r % NS
                        pe.wait_ge(S["out_ready"], b * PER["out_ready"] + r + 1)
                        if n == 0 and r > 0:
                            pe.wait_ge(S["y_read"], b * PER["y_read"] + r // NS)
                        for u in range(U):
                            for q in range(2):
                                x = mm(PS[:, 2 * u + q, 0:TQ], identf, outs[:, r % OUTS, u, q * TQ:(q + 1) * TQ],
                                       start=(n == 0), stop=(n == NS - 1))
                        x.then_inc(S["y_sum"], 1)

                    for r in range(32 * l, 32 * l + 32):
                        k, n = (r // NS) % 2, r % NS
                        t0 = k * TH
                        if r > 0:
                            pe.wait_ge(S["input_ready"], b * PER["input_ready"] + r)
                        for q in range(2):
                            x = mm(PS[:, 4 + q, 0:TQ], pick[:, n, :], bc_parts[0:96, t0 + q * TQ:t0 + (q + 1) * TQ],
                                   start=True, stop=True)
                        x.then_inc(S["b_bcast"], 1)
                        if r > 0:
                            pe.wait_ge(S["c_copied"], b * PER["c_copied"] + r)
                        for q in range(2):
                            x = mm(PS[:, 6 + q, 0:TQ], pick[:, NS + n, :], bc_parts[0:96, t0 + q * TQ:t0 + (q + 1) * TQ],
                                   start=True, stop=True)
                        x.then_inc(S["c_bcast"], 1)
                        if r >= 32 * l + LAG:
                            accumulate(r - LAG)
                    for r in range(32 * l + 32 - LAG, 32 * l + 32):
                        accumulate(r)
                    pe.wait_ge(S["gated"], b * PER["gated"] + 2 * l + 2)
                    pe.wait_ge(S["y_read"], b * PER["y_read"] + 2 * l + 2)
                    dense(0, [(wo[:, l, u, :], gate[:, u, :]) for u in range(U)]).then_inc(S["wo_sum"], 1)
                    layer_norm(l + 1, res, "ln_src", l + 2)

                layer_norm(3, h0, "ln_src", 4)

                def router():
                    pe.wait_ge(S["pooled"], b * PER["pooled"] + 1)
                    mm(PS[:, 6, 0:1], w("r_w1"), small[:, 0:1], start=True, stop=True).then_inc(S["r_hidden_sum"], 1)
                    pe.wait_ge(S["r_bcast"], b * PER["r_bcast"] + 1)
                    mm(PS[:, 7, 0:2 * EXP], hidden_bc, w("r_w2"), start=True, stop=True).then_inc(S["r_sum"], 1)

                layer_norm(4, res, "ln_out", 4, router)

                for a in range(ATT):
                    if a == 0:
                        pe.wait_ge(S["chosen"], b * PER["chosen"] + 1)
                        pe.wait_ge(S["att_in"], b * PER["att_in"] + 1)
                    else:
                        pe.wait_ge(S["att_in"], b * PER["att_in"] + 2)
                        pe.wait_ge(S["att_out"], b * PER["att_out"] + a)
                    dense(0, [(aw(a, "q"), att_q(a))]).then_inc(S["q_sum"], 1)
                    dense(1, [(aw(a, "k"), att_kv(a))]).then_inc(S["k_sum"], 1)
                    pe.wait_ge(S["q_read"], b * PER["q_read"] + a + 1)
                    for k in range(NB):
                        x = mm(PS[:, k // 3, (k % 3) * P:(k % 3 + 1) * P], att_kv(a)[:, k * P:(k + 1) * P],
                               aw(a, "v"), start=True, stop=True)
                    x.then_inc(S["v_sum"], 1)

                    pe.wait_ge(S["v_read"], b * PER["v_read"] + a + 1)
                    pe.wait_ge(S["k_read"], b * PER["k_read"] + a + 1)
                    pe.wait_ge(S["k_stacks_in"], b * PER["k_stacks_in"] + 96 * (a + 1))
                    keep_warm(24)
                    pe.wait_ge(S["q_stacks_in"], b * PER["q_stacks_in"] + 96 * (a + 1))
                    units, tops = score_units(a == 1), max_units(a == 1)
                    top0, unit0 = sum(N_MAX[:a]), sum(N_SCORES[:a])
                    for what, pair, *rest in ORDER[a]:
                        if what == "max":
                            j, qb, c = tops[rest[0]]
                            h, m = 2 * pair + j, top0 + pair * len(tops) + rest[0]
                            if pair > 0 and rest[0] < 3:
                                pe.wait_ge(S["max_rows"], b * PER["max_rows"] + PAIRS * a + pair)
                            before = bank_before(m, top0)
                            if before is not None:
                                if COPIED[before]:
                                    pe.wait_ge(S["max_copied"], b * PER["max_copied"] + COPIES[before + 1])
                                else:
                                    pe.wait_ge(S["max_read"], b * PER["max_read"] + READS[before + 1])
                            cols = min(C3, P * (qb + 1) - C3 * c) if a == 1 else C3
                            diag = a == 1 and c == qb // 3
                            dst = PS[:, MAX_BANK[m], 0:cols]
                            x = mm(dst, q_stack[0:KQ, h, qb * P:(qb + 1) * P],
                                   k_stack[0:KQ, h, c * C3:c * C3 + cols], start=True, stop=not diag)
                            if diag:
                                x = mm(dst[:, cols - P:cols], ident, mask_q, start=False, stop=True)
                            x.then_inc(S["max_scores"], 1)
                        elif what == "turn":
                            pe.wait_ge(S["max_split"], b * PER["max_split"] + PAIRS * a + pair + 1)
                            for k in range(NB):
                                x = mm(PS[0:6, 5 + k // 3, (k % 3) * P:(k % 3 + 1) * P],
                                       max_parts[:, pair, k, :, :].rearrange("p s h -> p (s h)"), ident,
                                       start=True, stop=True)
                            x.then_inc(S["max_turned"], 1)
                            if pair == 0:
                                keep_warm(20)
                        elif what == "exp":
                            i = rest[0]
                            qc, kb = units[i]
                            n = unit0 + pair * len(units) + i
                            if i == 0:
                                pe.wait_ge(S["max_rows_in"], b * PER["max_rows_in"] + 48 * (PAIRS * a + pair + 1))
                                if a == 0 and pair == 0:
                                    pe.wait_ge(S["ones_ready"], b * PER["ones_ready"] + 1)
                                    pe.wait_ge(S["ones_in"], b * PER["ones_in"] + 16)
                            before = scores_before(n, unit0)
                            if before is not None:
                                pe.wait_ge(S["weights"], b * PER["weights"] + before + 1)
                            s = max(0, P * kb - C3 * qc) if a == 1 else 0
                            diag = a == 1 and kb >= 3 * qc
                            for j in range(2):
                                h, bank = 2 * pair + j, SCORE_BANKS[n] + j
                                x = mm(PS[:, bank, s:C3], k_stack[0:KQ + 3, h, kb * P:(kb + 1) * P],
                                       q_stack[0:KQ + 3, h, qc * C3 + s:(qc + 1) * C3], start=True, stop=not diag)
                                if diag:
                                    x = mm(PS[:, bank, s:s + P], ident, mask_k, start=False, stop=True)
                            x.then_inc(S["scores"], 1)
                        elif what == "weigh":
                            i = rest[0]
                            qc, kb = units[i]
                            n = unit0 + pair * len(units) + i
                            reads = 3 * PAIRS * a + 3 * pair + qc
                            pe.wait_ge(S["weights"], b * PER["weights"] + n + 1)
                            if kb == 0 and reads > 3 * PAIRS * a:
                                pe.wait_ge(S["heads_read"], b * PER["heads_read"] + reads)
                            s = max(0, P * kb - C3 * qc) if a == 1 else 0
                            keys = min(NB, 3 * qc + 3) if a == 1 else NB
                            sets = halves(a == 1, qc)
                            for j in range(2):
                                o = 64 * (kb % sets) + 32 * j
                                x = mm(PS[o:o + 32, 4, s:C3], v_aug[:, kb, 2 * pair + j, :], wts[n % 4][:, j, s:C3],
                                       start=(kb < sets), stop=(kb >= keys - sets))
                            x.then_inc(S["weights_used"], 1)
                    pe.wait_ge(S["heads_read"], b * PER["heads_read"] + 3 * PAIRS * (a + 1))
                    for g in range(2):
                        for k in range(NB):
                            o = 4 * (NB * g + k)
                            x = mm(PS[:, 6, o:o + 4], heads_o[:, g, k * P:(k + 1) * P], sum_row[:, 0:4],
                                   start=True, stop=True)
                    x.then_inc(S["denom"], 1)
                    pe.wait_ge(S["denom_inv"], b * PER["denom_inv"] + a + 1)
                    for g in range(2):
                        for k in range(NB):
                            o = 4 * (NB * g + k)
                            x = mm(PS[:, 3 * g + k // 3, (k % 3) * P:(k % 3 + 1) * P],
                                   inverse_rows[:, 32 * o:32 * o + P], identf, start=True, stop=True)
                        x.then_inc(S["denom_bcast"], 1)
                    pe.wait_ge(S["heads_out"], b * PER["heads_out"] + 2 * a + 2)
                    dense(0, [(aw(a, "o0"), heads_o[:, 0, :]), (aw(a, "o1"), heads_o[:, 1, :])]).then_inc(S["proj_sum"], 1)

                layer_norm(5, res, "ln_src", 5)
                pe.wait_ge(S["ln_out"], b * PER["ln_out"] + 6)
                for m in range(4):
                    if m >= 2:
                        pe.wait_ge(S["mlp_hidden"], b * PER["mlp_hidden"] + m - 1)
                    dense(m % 2, [(w("m_w1")[:, m * P:(m + 1) * P], xhat)]).then_inc(S["mlp_sum"], 1)
                pe.wait_ge(S["mlp_hidden"], b * PER["mlp_hidden"] + 4)
                dense(0, [(w("m_w2")[:, m * P:(m + 1) * P], hidden[:, m, :]) for m in range(4)]).then_inc(S["mlp_out_sum"], 1)

        @block.scalar
        def _(act):
            A = nc.scalar.activation
            act.wait_ge(loaded, 48)
            A(a_neg[:, :], w("a_log"), ACT.Exp).then_inc(decays_ready, 1)
            act.wait_ge(decays_ready, 2)
            with act.Fori(0, B) as b:
                def layer_norm(i):
                    act.wait_ge(S["ln_centered"], b * PER["ln_centered"] + i + 1)
                    A(sq[:, :], cen[:, :], ACT.Square).then_inc(S["ln_squared"], 1)
                    act.wait_ge(S["ln_var"], b * PER["ln_var"] + i + 1)
                    A(deviation, PS[:, 6, 0:NB], ACT.Sqrt, bias=w("eps")).then_inc(S["ln_std"], 1)

                layer_norm(0)
                for l in range(L):
                    def silu_z(u):
                        act.wait_ge(S["z_sum"], b * PER["z_sum"] + 2 * l + u + 1)
                        A(banks3(zs[:, u, :]), slot(1), ACT.Silu).then_inc(S["zs_ready"], 1)

                    for u in range(U):
                        act.wait_ge(S["xc_sum"], b * PER["xc_sum"] + 2 * l + u + 1)
                        A(banks3(xs[:, u, :]), slot(u), ACT.Silu, bias=w("conv_b")[:, 2 * l + u:2 * l + u + 1]).then_inc(S["xs_ready"], 1)
                    act.wait_ge(S["dbc_sum"], b * PER["dbc_sum"] + l + 1)
                    A(banks3(dt_rows[96:96 + RANK, :]), slot(0)[96:96 + RANK], ACT.Copy).then_inc(S["dt_rows"], 1)
                    A(banks3(bc_hi[0:96, :]), slot(0)[0:96], ACT.Copy).then_inc(S["bc_hi"], 1)
                    silu_z(0)
                    act.wait_ge(S["bc_rest"], b * PER["bc_rest"] + l + 1)
                    A(bc_mid[0:96, :], bc_rest[0:96, :], ACT.Copy).then_inc(S["bc_mid"], 1)
                    for u in range(U):
                        act.wait_ge(S["dt_sum"], b * PER["dt_sum"] + 2 * l + u + 1)
                        A(banks3(gate[:, u, :]), slot(1 - u), ACT.Abs, bias=w("bdt")[:, 2 * l + u:2 * l + u + 1]).then_inc(S["dt_abs"], 1)
                        act.wait_ge(S["dt_abs"], b * PER["dt_abs"] + 2 * l + u + 1)
                        A(dx[:, u, :], gate[:, u, :], ACT.Exp, scale=-1.0).then_inc(S["dt_exp"], 1)
                        act.wait_ge(S["dt_exp"], b * PER["dt_exp"] + 2 * l + u + 1)
                        A(gate[:, u, :], dx[:, u, :], ACT.Ln, bias=1.0).then_inc(S["dt_log"], 1)
                    silu_z(1)
                    act.wait_ge(S["delta_ready"], b * PER["delta_ready"] + 2 * l + 2)
                    for r in range(32 * l, 32 * l + 32):
                        k, n = (r // NS) % 2, r % NS
                        t0 = k * TH
                        if r >= 2:
                            act.wait_ge(S["state_ready"], b * PER["state_ready"] + 2 * (r - 1))
                        for u in range(U):
                            col = (l * U + u) * NS + n
                            A(decay[:, r % 2, u, :], delta[:, u, t0:t0 + TH], ACT.Exp,
                                 scale=a_neg[:, col:col + 1]).then_inc(S["decay_ready"], 1)
                        act.wait_ge(S["c_bcast"], b * PER["c_bcast"] + r + 1)
                        if r >= 3:
                            act.wait_ge(S["out_ready"], b * PER["out_ready"] + r - 2)
                        A(c_sb[:, r % 3, :].rearrange("p (q t) -> p q t", q=2), PS[:, 6:8, 0:TQ], ACT.Copy).then_inc(S["c_copied"], 1)
                    layer_norm(l + 1)
                layer_norm(3)
                act.wait_ge(S["r_hidden_sum"], b * PER["r_hidden_sum"] + 1)
                A(small[:, 1:2], PS[:, 6, 0:1], ACT.Gelu, bias=w("r_b1")).then_inc(S["r_hidden"], 1)
                layer_norm(4)
                for a in range(ATT):
                    act.wait_ge(S["k_sum"], b * PER["k_sum"] + a + 1)
                    A(banks3(qf), slot(1), ACT.Identity, bias=aw(a, "kb")).then_inc(S["k_read"], 1)
                    act.wait_ge(S["k_read"], b * PER["k_read"] + a + 1)
                    A(k_parts[:, 0, :], qf, ACT.Copy).then_inc(S["k_hi"], 1)
                    act.wait_ge(S["k_rest"], b * PER["k_rest"] + a + 1)
                    A(k_parts[:, 1, :], sq[:, :], ACT.Copy).then_inc(S["k_mid"], 1)
                    act.wait_ge(S["q_read"], b * PER["q_read"] + a + 1)
                    A(q_parts[:, 0, :], cen[:, :], ACT.Copy).then_inc(S["q_hi"], 1)
                    act.wait_ge(S["q_rest"], b * PER["q_rest"] + a + 1)
                    A(q_parts[:, 1, :], rstd[:, :], ACT.Copy).then_inc(S["q_mid"], 1)
                    units, unit0 = score_units(a == 1), sum(N_SCORES[:a])
                    tops, top0 = max_units(a == 1), sum(N_MAX[:a])
                    for what, pair, *rest in ORDER[a]:
                        if what == "max":
                            m = top0 + pair * len(tops) + rest[0]
                            if COPIED[m]:
                                act.wait_ge(S["max_scores"], b * PER["max_scores"] + m + 1)
                                if GROUPS[m] >= 2:
                                    act.wait_ge(S["tops_kept"], b * PER["tops_kept"] + GROUPS[m] - 1)
                                A(top_slot(m, tops[rest[0]][1]), PS[:, MAX_BANK[m], 0:C3], ACT.Copy).then_inc(S["max_copied"], 1)
                        elif what == "rows":
                            act.wait_ge(S["max_turned"], b * PER["max_turned"] + PAIRS * a + pair + 1)
                            if pair > 0:
                                act.wait_ge(S["max_rows_in"], b * PER["max_rows_in"] + 48 * (PAIRS * a + pair))
                            A(banks3(max_rows[0:6, :]), PS[0:6, 5:8, 0:C3], ACT.Copy).then_inc(S["max_rows"], 1)
                        elif what == "read" and halves(a == 1, rest[0]) == 2:
                            done = sum(1 for u in units if u[0] <= rest[0])
                            reads = 3 * PAIRS * a + 3 * pair + rest[0]
                            act.wait_ge(S["weights_used"], b * PER["weights_used"] + unit0 + pair * len(units) + done)
                            if reads > 3 * PAIRS * a:
                                act.wait_ge(S["heads_read"], b * PER["heads_read"] + reads)
                            A(odd_sums[0:64, :], PS[64:128, 4, 0:C3], ACT.Copy).then_inc(S["heads_copied"], 1)
                        elif what == "exp":
                            qc, kb = units[rest[0]]
                            n = unit0 + pair * len(units) + rest[0]
                            s = max(0, P * kb - C3 * qc) if a == 1 else 0
                            act.wait_ge(S["scores"], b * PER["scores"] + n + 1)
                            if n >= unit0 + 4:
                                act.wait_ge(S["weights_used"], b * PER["weights_used"] + n - 3)
                            A(wts[n % 4][:, :, s:C3], PS[:, SCORE_BANKS[n]:SCORE_BANKS[n] + 2, s:C3], ACT.Exp).then_inc(S["weights"], 1)
                layer_norm(5)
                for m in range(4):
                    act.wait_ge(S["mlp_sum"], b * PER["mlp_sum"] + m + 1)
                    A(banks3(hidden[:, m, :]), slot(m % 2), ACT.Gelu, bias=w("m_b1")[:, m:m + 1]).then_inc(S["mlp_hidden"], 1)

        @block.vector
        def _(dve):
            tt, ts, stt = nc.vector.tensor_tensor, nc.vector.tensor_scalar, nc.vector.scalar_tensor_tensor
            dve.wait_ge(loaded, 48)
            nc.vector.tensor_copy(CB[:, :], consts_f32)
            for l in range(L):
                for j in range(TAPS):
                    x = tt(conv_wi[:, l, j, :], wi[:, l, 0:256], conv_w[:, l, j, :], ALU.mult)
            nc.vector.memset(h_pad[:, 0:3], 0.0).then_inc(convs_ready, 1)
            dve.wait_ge(convs_ready, 1)
            nc.vector.memset(k_stack[KQ:KQ + 3, :, :], 1.0).then_inc(convs_ready, 1)
            dve.wait_ge(decays_ready, 1)
            ts(a_neg[:, :], a_neg[:, :], -1.0, None, ALU.mult).then_inc(decays_ready, 1)
            with dve.Fori(0, B) as b:
                steps = [0]

                def step(instruction):
                    steps[0] += 1
                    instruction.then_inc(S["dve_step"], 1)
                    dve.wait_ge(S["dve_step"], b * PER["dve_step"] + steps[0])

                def layer_norm(i, src, dst, affine=None, meanwhile=None):
                    dve.wait_ge(S["ln_mean"], b * PER["ln_mean"] + i + 1)
                    tt(banks3(cen[:, :]), banks3(src), slot(0), ALU.subtract).then_inc(S["ln_centered"], 1)
                    if meanwhile:
                        meanwhile()
                    dve.wait_ge(S["ln_std"], b * PER["ln_std"] + i + 1)
                    r, v, t = stats[:, 0:NB], stats[:, NB:2 * NB], stats[:, 2 * NB:3 * NB]
                    ts(v, PS[:, 6, 0:NB], EPS, None, ALU.add)
                    step(nc.vector.reciprocal(r, deviation))
                    step(tt(t, r, r, ALU.mult))
                    step(tt(t, t, v, ALU.mult))
                    step(ts(t, t, -0.5, 1.5, ALU.mult, ALU.add))
                    tt(r, r, t, ALU.mult).then_inc(S["ln_rstd"], 1)
                    dve.wait_ge(S["ln_bcast"], b * PER["ln_bcast"] + i + 1)
                    if affine is None:
                        return tt(banks3(dst), banks3(cen[:, :]), slot(1), ALU.mult)
                    step(tt(banks3(dst), banks3(cen[:, :]), slot(1), ALU.mult))
                    return ts(dst, dst, affine[0], affine[1], ALU.mult, ALU.add)

                dve.wait_ge(S["tokens_in"], b * PER["tokens_in"] + 32)
                dve.wait_ge(S["result"], b * PER["result"])
                nc.vector.tensor_copy(h0[:, IMG:T], texts)
                dve.wait_ge(S["emb_sum"], b * PER["emb_sum"] + 1)
                pe_cols = w("pe")
                tt(h0[:, 0:2 * C3].rearrange("p (c t) -> p c t", c=2), PS[:, 0:2, 0:C3],
                   pe_cols[:, 0:2 * C3].rearrange("p (c t) -> p c t", c=2), ALU.add)
                tt(h0[:, 2 * C3:IMG], PS[:, 2, 0:IMG - 2 * C3], pe_cols[:, 2 * C3:IMG], ALU.add).then_inc(S["ln_src"], 1)
                dve.wait_ge(S["ln_src"], b * PER["ln_src"] + 1)
                layer_norm(0, h0[:, :], h_pad[:, 3:3 + T]).then_inc(S["ln_out"], 1)

                for l in range(L):
                    dve.wait_ge(S["bc_hi"], b * PER["bc_hi"] + l + 1)
                    stt(banks3(bc_rest[0:96, :]), banks3(bc_hi[0:96, :]), masks[0:96, 0:1], slot(0)[0:96],
                           ALU.mult, ALU.add).then_inc(S["bc_rest"], 1)
                    dve.wait_ge(S["bc_mid"], b * PER["bc_mid"] + l + 1)
                    stt(bc_parts[0:96, :], bc_mid[0:96, :], masks[0:96, 1:2], bc_rest[0:96, :],
                           ALU.mult, ALU.add).then_inc(S["bc_parts"], 1)
                    for u in range(U):
                        dve.wait_ge(S["dt_abs"], b * PER["dt_abs"] + 2 * l + u + 1)
                        ts(banks3(delta[:, u, :]), slot(1 - u), w("bdt")[:, 2 * l + u:2 * l + u + 1], 0.0,
                              ALU.add, ALU.max).then_inc(S["dt_read"], 1)
                    for u in range(U):
                        dve.wait_ge(S["dt_exp"], b * PER["dt_exp"] + 2 * l + u + 1)
                        e = dx[:, u, :]
                        if l == 0 and u == 0:
                            dve.wait_ge(S["stored"], b * PER["stored"])
                        ts(e_small, e, SMALL_E, None, ALU.is_lt)
                        ts(rstd[:, :], e, -0.5, 1.0, ALU.mult, ALU.add)
                        step(ts(sq[:, :], e, 1.0, 1.0, ALU.add, ALU.subtract))
                        tt(rstd[:, :], rstd[:, :], e, ALU.mult)
                        step(tt(sq[:, :], sq[:, :], e, ALU.subtract))
                        dve.wait_ge(S["dt_log"], b * PER["dt_log"] + 2 * l + u + 1)
                        step(tt(sq[:, :], gate[:, u, :], sq[:, :], ALU.subtract))
                        dve.sem_inc(S["log_waited"], 1)
                        step(nc.vector.copy_predicated(sq[:, :], e_small, rstd[:, :]))
                        tt(delta[:, u, :], delta[:, u, :], sq[:, :], ALU.add).then_inc(S["delta_ready"], 1)
                        dve.wait_ge(S["delta_ready"], b * PER["delta_ready"] + 2 * l + u + 1)
                        tt(dx[:, u, :], delta[:, u, :], xs[:, u, :], ALU.mult).then_inc(S["dx_ready"], 1)
                    dve.wait_ge(S["dx_ready"], b * PER["dx_ready"] + 2 * l + 2)

                    def drives(r):
                        t0 = ((r // NS) % 2) * TH
                        dve.wait_ge(S["b_bcast"], b * PER["b_bcast"] + r + 1)
                        if r >= 3:
                            dve.wait_ge(S["state_ready"], b * PER["state_ready"] + 2 * (r - 2))
                        bb = PS[:, 4:6, 0:TQ].unsqueeze(1).broadcast_to([P, U, 2, TQ])
                        tt(drive[r % 3].rearrange("p u (q t) -> p u q t", q=2),
                              dx[:, :, t0:t0 + TH].rearrange("p u (q t) -> p u q t", q=2), bb, ALU.mult).then_inc(S["input_ready"], 1)

                    def read_y(m):
                        t0 = (m % 2) * TH
                        dve.wait_ge(S["y_sum"], b * PER["y_sum"] + NS * (m + 1))
                        for u in range(U):
                            x = stt(gate[:, u, t0:t0 + TH].rearrange("p (q t) -> p q t", q=2),
                                    xs[:, u, t0:t0 + TH].rearrange("p (q t) -> p q t", q=2),
                                    w("d_skip")[:, 2 * l + u:2 * l + u + 1], PS[:, 2 * u:2 * u + 2, 0:TQ],
                                    ALU.mult, ALU.add)
                        x.then_inc(S["y_read"], 1)
                        dve.wait_ge(S["y_read"], b * PER["y_read"] + m + 1)
                        tt(gate[:, :, t0:t0 + TH], gate[:, :, t0:t0 + TH], zs[:, :, t0:t0 + TH], ALU.mult).then_inc(S["gated"], 1)

                    drives(32 * l)
                    for r in range(32 * l, 32 * l + 32):
                        k, n = (r // NS) % 2, r % NS
                        if r + 1 < 32 * l + 32:
                            drives(r + 1)
                        dve.wait_ge(S["decay_ready"], b * PER["decay_ready"] + 2 * r + 2)
                        dve.wait_ge(S["input_ready"], b * PER["input_ready"] + r + 1)
                        if r >= 3:
                            dve.wait_ge(S["out_ready"], b * PER["out_ready"] + r - 2)
                        for u in range(U):
                            init = 0.0 if k == 0 else last[:, u, n:n + 1]
                            nc.vector.tensor_tensor_scan(state[:, r % 3, u, :], decay[:, r % 2, u, :],
                                                            drive[r % 3][:, u, :], init, ALU.mult, ALU.add).then_inc(S["state_ready"], 1)
                        if k == 0:
                            dve.wait_ge(S["state_ready"], b * PER["state_ready"] + 2 * r + 2)
                            nc.vector.tensor_copy(last[:, :, n:n + 1], state[:, r % 3, :, TH - 1:TH]).then_inc(S["last_saved"], 1)
                            if n == NS - 1:
                                dve.wait_ge(S["last_saved"], b * PER["last_saved"] + NS * (l + 1))
                        if k == 1 and n == LAG - 1:
                            read_y(2 * l)
                    read_y(2 * l + 1)
                    dve.wait_ge(S["wo_sum"], b * PER["wo_sum"] + l + 1)
                    tt(banks3(res[:, :]), slot(0), banks3(h_pad[:, 3:3 + T]), ALU.add).then_inc(S["ln_src"], 1)
                    dve.wait_ge(S["ln_src"], b * PER["ln_src"] + l + 2)
                    g, bb = w("ln_g")[:, l:l + 1], w("ln_b")[:, l:l + 1]
                    layer_norm(l + 1, res[:, :], h_pad[:, 3:3 + T], (g, bb)).then_inc(S["ln_out"], 1)
                dve.wait_ge(S["ln_out"], b * PER["ln_out"] + 3)
                tt(h0[:, :], h0[:, :], h_pad[:, 3:3 + T], ALU.add).then_inc(S["ln_src"], 1)
                dve.wait_ge(S["ln_src"], b * PER["ln_src"] + 4)
                layer_norm(3, h0[:, :], res[:, :]).then_inc(S["ln_out"], 1)
                dve.wait_ge(S["ln_out"], b * PER["ln_out"] + 4)
                step(nc.vector.tensor_reduce(small[:, 2:3], res[:, :], AX.X, ALU.add))
                ts(small[:, 0:1], small[:, 2:3], 1.0 / T, None, ALU.mult).then_inc(S["pooled"], 1)

                def choose():
                    dve.wait_ge(S["r_hidden"], b * PER["r_hidden"] + 1)
                    nc.vector.tensor_copy(hidden_bc, small[:, 1:2].broadcast_to([P, P])).then_inc(S["r_bcast"], 1)
                    dve.wait_ge(S["r_sum"], b * PER["r_sum"] + 1)
                    lg = small[:, 8:16].rearrange("p (s e) -> p s e", s=2)
                    hot = small[:, 16:24].rearrange("p (s e) -> p s e", s=2)
                    top, free = small[:, 24:26], small[:, 26:28]
                    step(tt(small[:, 8:16], PS[:, 7, 0:2 * EXP], w("r_b2"), ALU.add))
                    step(nc.vector.tensor_reduce(top, lg, AX.X, ALU.max))
                    step(tt(hot, lg, top.unsqueeze(2).broadcast_to([P, 2, EXP]), ALU.is_ge))
                    step(ts(free, hot[:, :, 0], -1.0, 1.0, ALU.mult, ALU.add))
                    for e in range(1, EXP):
                        step(tt(hot[:, :, e], hot[:, :, e], free, ALU.mult))
                        if e < EXP - 1:
                            step(tt(free, free, hot[:, :, e], ALU.subtract))
                    for s in range(2):
                        cs = slice(s * AW, (s + 1) * AW)
                        step(ts(chosen[:, cs], expert[:, 0, cs], hot[:, s, 0:1], None, ALU.mult))
                        for e in range(1, EXP):
                            x = stt(chosen[:, cs], expert[:, e, cs], hot[:, s, e:e + 1], chosen[:, cs], ALU.mult, ALU.add)
                            if e < EXP - 1:
                                step(x)
                    x.then_inc(S["chosen"], 1)

                layer_norm(4, res[:, :], s_out, meanwhile=choose).then_inc(S["ln_out"], 1)
                dve.wait_ge(S["ln_out"], b * PER["ln_out"] + 5)
                ts(xhat, s_out, norms[:, 0:1], norms[:, 1:2], ALU.mult, ALU.add).then_inc(S["att_in"], 1)
                ts(t_in, s_out, norms[:, 2:3], norms[:, 3:4], ALU.mult, ALU.add).then_inc(S["att_in"], 1)

                for a in range(ATT):
                    dve.wait_ge(S["q_sum"], b * PER["q_sum"] + a + 1)
                    ts(banks3(cen[:, :]), slot(0), aw(a, "qb"), HD ** -0.5, ALU.add, ALU.mult).then_inc(S["q_read"], 1)
                    dve.wait_ge(S["k_hi"], b * PER["k_hi"] + a + 1)
                    tt(sq[:, :], qf, k_parts[:, 0, :], ALU.subtract).then_inc(S["k_rest"], 1)
                    dve.wait_ge(S["k_mid"], b * PER["k_mid"] + a + 1)
                    tt(k_parts[:, 2, :], sq[:, :], k_parts[:, 1, :], ALU.subtract).then_inc(S["k_parts"], 1)
                    dve.wait_ge(S["q_hi"], b * PER["q_hi"] + a + 1)
                    tt(rstd[:, :], cen[:, :], q_parts[:, 0, :], ALU.subtract).then_inc(S["q_rest"], 1)
                    dve.wait_ge(S["q_mid"], b * PER["q_mid"] + a + 1)
                    tt(q_parts[:, 2, :], rstd[:, :], q_parts[:, 1, :], ALU.subtract).then_inc(S["q_parts"], 1)
                    dve.wait_ge(S["v_sum"], b * PER["v_sum"] + a + 1)
                    vb = aw(a, "vb").rearrange("p (h c) -> p h c", h=HEADS)
                    for c in range(3):
                        for k in range(3):
                            x = tt(v_aug[:, 3 * c + k, :, 0:HD],
                                   PS[:, c, k * P:(k + 1) * P].rearrange("p (h c) -> p h c", h=HEADS), vb, ALU.add)
                    x.then_inc(S["v_read"], 1)
                    if a == 0:
                        nc.vector.memset(v_aug[:, :, :, HD:32], 1.0).then_inc(S["ones_ready"], 1)
                    units, tops = score_units(a == 1), max_units(a == 1)
                    top0, unit0 = sum(N_MAX[:a]), sum(N_SCORES[:a])
                    for what, pair, *rest in ORDER[a]:
                        if what == "max":
                            j, qb, c = tops[rest[0]]
                            m = top0 + pair * len(tops) + rest[0]
                            cols = min(C3, P * (qb + 1) - C3 * c) if a == 1 else C3
                            if COPIED[m]:
                                continue
                            dve.wait_ge(S["max_scores"], b * PER["max_scores"] + m + 1)
                            if COPIED[m - 1] and c == 1:
                                dve.wait_ge(S["max_copied"], b * PER["max_copied"] + COPIES[m])
                                top = top_slot(m - 1, qb)
                                nc.vector.tensor_tensor_scan(top, PS[:, MAX_BANK[m], 0:C3], top, -3e38, ALU.max,
                                                             ALU.max).then_inc(S["max_read"], 1)
                            else:
                                nc.vector.tensor_reduce(max3[:, pair, qb, j, c:c + 1], PS[:, MAX_BANK[m], 0:cols],
                                                        AX.X, ALU.max).then_inc(S["max_read"], 1)
                            if GROUP_ENDS[m]:
                                g0, k = qb - qb % 3, qb % 3 + 1
                                dve.wait_ge(S["max_read"], b * PER["max_read"] + READS[m])
                                ends = top_buffers[GROUPS[m] % 2].rearrange("p (k t) -> p k t", k=3)
                                nc.vector.tensor_copy(max3[:, pair, g0:g0 + k, j, 0:2],
                                                      ends[:, 0:k, C3 - 1:C3].broadcast_to([P, k, 2])
                                                      ).then_inc(S["tops_kept"], 1)
                        elif what == "split":
                            dve.wait_ge(S["max_read"], b * PER["max_read"] + READS[top0 + (pair + 1) * len(tops)])
                            dve.wait_ge(S["tops_kept"], b * PER["tops_kept"] + GROUPS[top0 + (pair + 1) * len(tops)])
                            for c in range(3):
                                ks = slice(3 * c, 3 * c + 3)
                                x = nc.vector.tensor_reduce(max_tmp[:, pair, ks, :],
                                                            max3[:, pair, ks, :, 0:(c + 1 if a == 1 else 3)],
                                                            AX.X, ALU.max)
                            step(x)
                            low, parts = max_tmp[:, pair], max_parts[:, pair]
                            step(ts(neg_max[:, pair], low, -1.0, None, ALU.mult))
                            step(nc.vector.tensor_copy(parts[:, :, 0, :], neg_max[:, pair]))
                            step(tt(low, neg_max[:, pair], parts[:, :, 0, :], ALU.subtract))
                            step(nc.vector.tensor_copy(parts[:, :, 1, :], low))
                            tt(parts[:, :, 2, :], low, parts[:, :, 1, :], ALU.subtract).then_inc(S["max_split"], 1)
                        elif what == "read":
                            qc = rest[0]
                            o = 64 * (pair % 2)
                            done = sum(1 for u in units if u[0] <= qc)
                            dve.wait_ge(S["weights_used"], b * PER["weights_used"] + unit0 + pair * len(units) + done)
                            dst = heads_o[o:o + 64, pair // 2, qc * C3:(qc + 1) * C3]
                            if halves(a == 1, qc) == 1:
                                nc.vector.tensor_copy(dst, PS[0:64, 4, 0:C3]).then_inc(S["heads_read"], 1)
                            else:
                                copies = READ_COPIES[3 * PAIRS * a + 3 * pair + qc] + 1
                                dve.wait_ge(S["heads_copied"], b * PER["heads_copied"] + copies)
                                tt(dst, PS[0:64, 4, 0:C3], odd_sums[0:64, :], ALU.add).then_inc(S["heads_read"], 1)
                    dve.wait_ge(S["denom"], b * PER["denom"] + a + 1)
                    step(nc.vector.reciprocal(inverse, PS[:, 6, 0:8 * NB]))
                    nc.vector.tensor_copy(inverse_rows.rearrange("p (h c) -> p h c", c=32),
                                             inverse.unsqueeze(2).broadcast_to([P, 8 * NB, 32])).then_inc(S["denom_inv"], 1)
                    for g in range(2):
                        dve.wait_ge(S["denom_bcast"], b * PER["denom_bcast"] + 2 * a + g + 1)
                        tt(banks3(heads_o[:, g, :]), banks3(heads_o[:, g, :]), slot(g), ALU.mult).then_inc(S["heads_out"], 1)
                    dve.wait_ge(S["proj_sum"], b * PER["proj_sum"] + a + 1)
                    if a == 0:
                        ts(banks3(s_out), slot(0), aw(a, "ob"), None, ALU.add).then_inc(S["att_out"], 1)
                    elif a == 1:
                        stt(banks3(t_out), slot(0), aw(a, "ob"), banks3(t_in), ALU.add, ALU.add).then_inc(S["att_out"], 1)
                    else:
                        stt(banks3(res[:, :]), slot(0), aw(a, "ob"), banks3(res[:, :]), ALU.add, ALU.add).then_inc(S["ln_src"], 1)
                dve.wait_ge(S["ln_src"], b * PER["ln_src"] + 5)
                layer_norm(5, res[:, :], xhat, (norms[:, 4:5], norms[:, 5:6])).then_inc(S["ln_out"], 1)
                step(tt(h0[:, :], h0[:, :], res[:, :], ALU.add))
                dve.wait_ge(S["mlp_out_sum"], b * PER["mlp_out_sum"] + 1)
                stt(banks3(result[:, :]), slot(0), w("m_b2"), banks3(h0[:, :]), ALU.add, ALU.add).then_inc(S["result"], 1)

        @block.gpsimd
        def _(pool):
            with pool.Fori(0, B) as b:
                for r in range(64):
                    pool.wait_ge(S["state_ready"], b * PER["state_ready"] + 2 * r + 2)
                    pool.wait_ge(S["c_copied"], b * PER["c_copied"] + r + 1)
                    if r >= OUTS:
                        pool.wait_ge(S["y_sum"], b * PER["y_sum"] + r - OUTS + 1)
                    cc = c_sb[:, r % 3, :].unsqueeze(1).broadcast_to([P, U, TH])
                    nc.gpsimd.tensor_tensor(outs[:, r % OUTS, :, :], state[:, r % 3, :, :], cc, ALU.mult).then_inc(S["out_ready"], 1)


def pack(i):
    f = {k: np.asarray(v) for k, v in i.items()}
    parts = {}
    bc = lambda v: np.broadcast_to(v, (P, v.size))
    tall = lambda v: np.pad(v, ((0, P - v.shape[0]), (0, 0)))
    cols = lambda v: np.ascontiguousarray(v.reshape(-1, P).T)
    parts["tok_w"] = tall(f["L0_tok_W"])
    pos = np.arange(2 * IMG, dtype=np.float32)[:, None]
    div = np.exp(np.arange(0, D, 2, dtype=np.float32) * (-math.log(10000.0) / D))
    pe = np.zeros((2 * IMG, D), np.float32)
    pe[:, 0::2], pe[:, 1::2] = np.sin(pos * div), np.cos(pos * div)
    parts["pe"] = pe[:IMG].T
    parts["wi"] = f["L0_attn_in_proj_w"].transpose(1, 0, 2).reshape(P, -1)
    parts["conv_w"] = bc(f["L0_attn_conv_w"][:, :, 0, :].transpose(0, 2, 1).reshape(-1))
    parts["conv_b"] = cols(f["L0_attn_conv_b"])
    wx = f["L0_attn_x_proj_w"]
    wx = np.concatenate([wx[:, :, RANK:]] * 3 + [wx[:, :, :RANK]], axis=2)
    parts["wx"] = wx.reshape(L, U, P, SR).transpose(2, 0, 1, 3).reshape(P, -1)
    wdt = f["L0_attn_dt_proj_w"].transpose(1, 0, 2).reshape(RANK, -1)
    parts["wdt"] = np.pad(wdt, ((96, P - 96 - RANK), (0, 0)))
    parts["bdt"] = cols(f["L0_attn_dt_proj_b"])
    parts["a_log"] = f["L0_attn_A_log"].reshape(L, U, P, NS).transpose(2, 0, 1, 3).reshape(P, -1)
    parts["d_skip"] = cols(f["L0_attn_D_skip"])
    parts["wo"] = f["L0_attn_out_proj_w"].reshape(L, U, P, D).transpose(2, 0, 1, 3).reshape(P, -1)
    parts["ln_g"], parts["ln_b"] = f["L0_attn_ln_g"].T, f["L0_attn_ln_b"].T
    parts["r_w1"] = f["L0_ffn_router_w1"].T
    parts["r_b1"] = f["L0_ffn_router_b1"][:, None]
    parts["r_w2"] = f["L0_ffn_router_w2"].T
    parts["r_b2"] = bc(f["L0_ffn_router_b2"])
    parts["norms"] = np.stack([f["L0_ffn_" + n] for n in ("norm_s_w", "norm_s_b", "norm_t_w", "norm_t_b",
                                                          "norm_mlp_w", "norm_mlp_b")], axis=1)

    def attention(wq, wk, wv, bq, bk, bv, w_out, b_out):
        o = np.zeros((2, 4, 32, P), np.float32)
        o[:, :, :HD, :] = w_out.T.reshape(2, 4, HD, P)
        o = o.reshape(2 * P, P)
        return np.concatenate([wq.T, wk.T, wv.T, bc(bv), o[:P], o[P:], bq[:, None], bk[:, None], b_out[:, None]], 1)

    sides = []
    for e in range(EXP):
        win, bin_ = f["L0_ffn_sp_in_w"][e], f["L0_ffn_sp_in_b"][e]
        sides.append(attention(win[:D], win[D:2 * D], win[2 * D:], bin_[:D], bin_[D:2 * D], bin_[2 * D:],
                               f["L0_ffn_sp_out_w"][e], f["L0_ffn_sp_out_b"][e]))
        sides.append(attention(*(f[f"L0_ffn_t{n}_w"][e] for n in "qkv"), *(f[f"L0_ffn_t{n}_b"][e] for n in "qkv"),
                               f["L0_ffn_tp_w"][e], f["L0_ffn_tp_b"][e]))
    parts["expert"] = np.concatenate(sides, axis=1)
    win, bin_ = f["L0_ffn_cross_in_w"], f["L0_ffn_cross_in_b"]
    parts["cross"] = attention(win[:D], win[D:2 * D], win[2 * D:], bin_[:D], bin_[D:2 * D], bin_[2 * D:],
                               f["L0_ffn_cross_out_w"], f["L0_ffn_cross_out_b"])
    parts["m_w1"] = f["L0_ffn_mlp_w1"].T
    parts["m_b1"] = cols(f["L0_ffn_mlp_b1"])
    parts["m_w2"] = f["L0_ffn_mlp_w2"].T.reshape(4, P, D).transpose(1, 0, 2).reshape(P, -1)
    parts["m_b2"] = f["L0_ffn_mlp_b2"][:, None]
    parts["mean_mat"] = np.full((P, P), 1.0 / D, np.float32)
    parts["identf"] = np.eye(P, dtype=np.float32)
    sum_row = np.zeros((P, 4), np.float32)
    for h in range(4):
        sum_row[32 * h + HD, h] = 1.0
    parts["sum_row"] = sum_row
    masks = np.zeros((P, 2), np.float32)
    masks[32:, 0] = -1.0
    masks[64:, 1] = -1.0
    parts["masks"] = masks
    parts["eps"] = np.full((P, 1), EPS, np.float32)
    out = np.concatenate([parts[n] for n, _ in _F32], axis=1)
    assert out.shape == (P, F32_COLS) and out.dtype == np.float32
    return np.ascontiguousarray(out)


def constants():
    pick = np.zeros((P, 2 * NS, P), np.float32)
    for n in range(2 * NS):
        pick[[n, 32 + n, 64 + n], n, :] = 1.0
    late = np.triu(np.full((P, P), -1e38, np.float32), 1)
    return np.concatenate([np.eye(P, dtype=np.float32), late, late.T, pick.reshape(P, -1)], axis=1)


def kernel(**inputs):
    import concourse.bacc as _bacc
    from concourse.bass_utils import run_bass_kernel_spmd as _run

    B = inputs["x"].shape[0]
    arrays = {
        "xT": np.ascontiguousarray(np.asarray(inputs["x"]).reshape(B, IMG, FEAT).transpose(0, 2, 1)),
        "txtT": np.ascontiguousarray(np.asarray(inputs["txt"]).transpose(0, 2, 1)),
        "params": pack({k: v for k, v in inputs.items() if k not in ("x", "txt")}),
        "consts": constants(),
    }
    nc = _bacc.Bacc("TRN2", target_bir_lowering=False, num_devices=1)
    args = [nc.dram_tensor(n, a.shape, mybir.dt.from_np(a.dtype), kind="ExternalInput").ap()
            for n, a in arrays.items()]
    out = nc.dram_tensor("outT", (B, D, T), mybir.dt.float32, kind="ExternalOutput").ap()
    fusion_kernel(nc, *args, out)
    r = _run(nc, [arrays], core_ids=[0])
    return np.ascontiguousarray(r.results[0]["outT"].transpose(0, 2, 1))
```
